# Optimizing a Trainium2 kernel written in Bass

```python
import numpy as np
import jax
import jax.numpy as jnp

def _softmax(x, axis=-1):
    return jax.nn.softmax(x, axis=axis)

def _gelu(x):
    return jax.nn.gelu(x, approximate=True)

def _silu(x):
    return jax.nn.silu(x)

def _sigmoid(x):
    return jax.nn.sigmoid(x)

def _layernorm(x, axis=-1, eps=1e-05):
    m = jnp.mean(x, axis=axis, keepdims=True)
    v = jnp.var(x, axis=axis, keepdims=True)
    return (x - m) / jnp.sqrt(v + eps)

def _scatter_add(tgt, idx, src, axis=0):
    return tgt.at[idx].add(src)

def _segment_sum(src, seg, n):
    return jax.ops.segment_sum(src, seg, n)
kernel_name = 'mk_adaln_d1_jaxref_r8_ff7227'

def setup_inputs(seed: int=0):
    np.random.seed(seed)
    _w = jnp.asarray

    def _L0_attn_setup():
        import jax, jax.numpy as jnp
        import numpy as np
        B_, L_, DM, DIN, DXB, DS, DC, DTR = (2, 512, 256, 512, 128, 16, 4, 128)
        key = jax.random.key(seed)
        ks = jax.random.split(key, 12)
        s = lambda k, shape, sc=0.02: jax.random.normal(k, shape, jnp.float32) * sc
        dt = jnp.exp(jax.random.uniform(ks[9], (DIN,), jnp.float32) * (np.log(0.1) - np.log(0.001)) + np.log(0.001))
        bdt = dt + jnp.log(-jnp.expm1(-dt))
        A_log = jnp.log(jnp.tile(jnp.arange(1, DS + 1, dtype=jnp.float32), (DIN, 1)))
        return {'hidden_states': jax.random.normal(ks[0], (B_, L_, DM), jnp.float32), 'Wx': s(ks[1], (DXB, DM)), 'bx': jnp.zeros((DXB,), jnp.float32), 'Wz': s(ks[2], (DIN, DM)), 'bz': jnp.zeros((DIN,), jnp.float32), 'conv_w': s(ks[3], (DIN, 1, DC), 0.2), 'conv_b': jnp.zeros((DIN,), jnp.float32), 'WB': s(ks[4], (DXB, DM)), 'WC': s(ks[5], (DIN, DM)), 'Wdt_down': s(ks[6], (DTR, DM)), 'Wdt': s(ks[7], (DIN, DTR), DTR ** (-0.5)), 'bdt': bdt, 'A_log': A_log, 'D': jnp.ones((DIN,), jnp.float32), 'Wout': s(ks[8], (DM, DIN)), 'bout': jnp.zeros((DM,), jnp.float32)}
    _L0_attn_in = _L0_attn_setup()

    def _L0_ffn_setup():
        import jax, jax.numpy as jnp
        import numpy as np
        NUM_EXPERTS = 8
        TOP_K = 2
        EMB = 256
        MLP = 512
        B, S = (4, 128)
        key = jax.random.key(seed)
        ks = jax.random.split(key, 5)
        scale_x = 1.0
        return {'x': jax.random.normal(ks[0], (B, S, EMB), dtype=jnp.float32), 'gate_kernel': jax.random.normal(ks[1], (EMB, NUM_EXPERTS), dtype=jnp.float32) / np.sqrt(EMB), 'w0_kernel': jax.random.normal(ks[2], (NUM_EXPERTS, EMB, MLP), dtype=jnp.float32) / np.sqrt(EMB), 'w1_kernel': jax.random.normal(ks[3], (NUM_EXPERTS, EMB, MLP), dtype=jnp.float32) / np.sqrt(EMB), 'wo_kernel': jax.random.normal(ks[4], (NUM_EXPERTS, MLP, EMB), dtype=jnp.float32) / np.sqrt(MLP)}
    _L0_ffn_in = _L0_ffn_setup()
    _L0_c = _w((lambda *s: np.random.randn(*s).astype(np.float32) * 0.05)(2, 256))
    _L0_wmod = _w((lambda *s: np.random.randn(*s).astype(np.float32) * 0.05)(256, 6 * 256) * 256 ** (-0.5))
    _d = {'L0_attn_hidden_states': _L0_attn_in['hidden_states'], 'L0_attn_Wx': _L0_attn_in['Wx'], 'L0_attn_bx': _L0_attn_in['bx'], 'L0_attn_Wz': _L0_attn_in['Wz'], 'L0_attn_bz': _L0_attn_in['bz'], 'L0_attn_conv_w': _L0_attn_in['conv_w'], 'L0_attn_conv_b': _L0_attn_in['conv_b'], 'L0_attn_WB': _L0_attn_in['WB'], 'L0_attn_WC': _L0_attn_in['WC'], 'L0_attn_Wdt_down': _L0_attn_in['Wdt_down'], 'L0_attn_Wdt': _L0_attn_in['Wdt'], 'L0_attn_bdt': _L0_attn_in['bdt'], 'L0_attn_A_log': _L0_attn_in['A_log'], 'L0_attn_D': _L0_attn_in['D'], 'L0_attn_Wout': _L0_attn_in['Wout'], 'L0_attn_bout': _L0_attn_in['bout'], 'L0_ffn_gate_kernel': _L0_ffn_in['gate_kernel'], 'L0_ffn_w0_kernel': _L0_ffn_in['w0_kernel'], 'L0_ffn_w1_kernel': _L0_ffn_in['w1_kernel'], 'L0_ffn_wo_kernel': _L0_ffn_in['wo_kernel'], 'L0_c': _L0_c, 'L0_wmod': _L0_wmod}
    _x0 = _d['L0_attn_hidden_states']
    _d['L0_attn_hidden_states'] = jax.random.normal(jax.random.fold_in(jax.random.key(seed), 1), (2, 1024, 256), dtype=_x0.dtype)
    del _x0
    return _d

def reference(L0_attn_hidden_states, L0_attn_Wx, L0_attn_bx, L0_attn_Wz, L0_attn_bz, L0_attn_conv_w, L0_attn_conv_b, L0_attn_WB, L0_attn_WC, L0_attn_Wdt_down, L0_attn_Wdt, L0_attn_bdt, L0_attn_A_log, L0_attn_D, L0_attn_Wout, L0_attn_bout, L0_ffn_gate_kernel, L0_ffn_w0_kernel, L0_ffn_w1_kernel, L0_ffn_wo_kernel, L0_c, L0_wmod):

    def _L0_attn_ref(hidden_states, Wx, bx, Wz, bz, conv_w, conv_b, WB, WC, Wdt_down, Wdt, bdt, A_log, D, Wout, bout):
        import jax, jax.numpy as jnp
        import numpy as np
        B_, L_, DM, DIN, DXB, DS, DC, DTR = (2, 512, 256, 512, 128, 16, 4, 128)
        b, l, dm = hidden_states.shape
        din, ds = A_log.shape
        dxb = Wx.shape[0]
        nBh = dxb // ds
        nCh = din // ds
        ng = nCh // nBh
        ch = din // nCh
        x = hidden_states @ Wx.T + bx
        z = hidden_states @ Wz.T + bz
        A = -jnp.exp(A_log)
        Bm = (hidden_states @ WB.T).reshape(b, l, nBh, ds)
        Bm = jnp.repeat(Bm, ng, axis=2)
        Cm = (hidden_states @ WC.T).reshape(b, l, nCh, ds)
        dt_lin = hidden_states @ Wdt_down.T @ Wdt.T + bdt
        delta = jax.nn.softplus(dt_lin + bdt)
        x = jnp.repeat(x.reshape(b, l, nBh, ds), ng, axis=2).reshape(b, l, din)
        xc = x.transpose(0, 2, 1)
        xc = jax.lax.conv_general_dilated(xc, conv_w, (1,), [(DC - 1, 0)], dimension_numbers=('NCH', 'OIH', 'NCH'), feature_group_count=din)
        u = jax.nn.silu(xc + conv_b[None, :, None]).transpose(0, 2, 1)
        u_t = u.transpose(1, 0, 2)
        d_t = delta.transpose(1, 0, 2)
        B_t = Bm.transpose(1, 0, 2, 3)
        C_t = Cm.transpose(1, 0, 2, 3)

        def step(h, inp):
            ut, dt_, bt, ct = inp
            dA = jnp.exp(dt_[..., None] * A)
            dBu = ((dt_ * ut).reshape(b, nCh, ch, 1) * bt[:, :, None, :]).reshape(b, din, ds)
            h = dA * h + dBu
            y = (h.reshape(b, nCh, ch, ds) * ct[:, :, None, :]).sum(-1).reshape(b, din)
            return (h, y)
        h0 = jnp.zeros((b, din, ds), hidden_states.dtype)
        _, ys = jax.lax.scan(step, h0, (u_t, d_t, B_t, C_t))
        y = ys.transpose(1, 0, 2)
        y = (y + u * D) * jax.nn.silu(z)
        return y @ Wout.T + bout

    def _L0_ffn_ref(x, gate_kernel, w0_kernel, w1_kernel, wo_kernel):
        import jax, jax.numpy as jnp
        import numpy as np
        NUM_EXPERTS = 8
        TOP_K = 2
        EMB = 256
        MLP = 512
        B, S = (4, 128)
        gate_logits = jnp.einsum('bsd,de->bse', x, gate_kernel)
        top_k_weights, top_k_indices = jax.lax.top_k(gate_logits, TOP_K)
        top_k_weights = jax.nn.softmax(top_k_weights.astype(jnp.float32), axis=-1).astype(x.dtype)
        one_hot = jax.nn.one_hot(top_k_indices, NUM_EXPERTS, dtype=x.dtype)
        combine = jnp.einsum('bsk,bske->bse', top_k_weights, one_hot)
        h0 = jnp.einsum('bsd,edm->bsem', x, w0_kernel)
        h1 = jnp.einsum('bsd,edm->bsem', x, w1_kernel)
        inter = jax.nn.silu(h0) * h1
        out = jnp.einsum('bse,bsem,emd->bsd', combine, inter, wo_kernel)
        return out
    x = L0_attn_hidden_states
    mod = (_silu(L0_c) @ L0_wmod).reshape(L0_c.shape[0], 6, 1, -1)
    sa, ca, ga, sb, cb, gb = (mod[:, 0], mod[:, 1], mod[:, 2], mod[:, 3], mod[:, 4], mod[:, 5])
    ga = (2 * (ga >= 0) - 1) * jnp.maximum(jnp.abs(ga), 0.25)
    gb = (2 * (gb >= 0) - 1) * jnp.maximum(jnp.abs(gb), 0.25)
    h = _layernorm(x, axis=-1) * (1 + ca) + sa
    x = x + ga * _L0_attn_ref(h, L0_attn_Wx, L0_attn_bx, L0_attn_Wz, L0_attn_bz, L0_attn_conv_w, L0_attn_conv_b, L0_attn_WB, L0_attn_WC, L0_attn_Wdt_down, L0_attn_Wdt, L0_attn_bdt, L0_attn_A_log, L0_attn_D, L0_attn_Wout, L0_attn_bout)
    h = _layernorm(x, axis=-1) * (1 + cb) + sb
    x = x + gb * _L0_ffn_ref(h, L0_ffn_gate_kernel, L0_ffn_w0_kernel, L0_ffn_w1_kernel, L0_ffn_wo_kernel)
    return x

_drawn_inputs = setup_inputs


def setup_inputs(seed=0):
    import zlib

    import numpy as np

    out = dict(_drawn_inputs(seed))
    spreads = {'L0_attn_bx': (0.0, 0.8),
     'L0_attn_bz': (0.0, 0.8),
     'L0_attn_conv_b': (0.0, 0.8),
     'L0_attn_D': (1.0, 0.6),
     'L0_attn_bout': (0.0, 2.0)}
    factors = {'L0_attn_Wx': 8.0,
     'L0_attn_Wz': 8.0,
     'L0_attn_conv_w': 8.0,
     'L0_attn_WB': 8.0,
     'L0_attn_WC': 8.0,
     'L0_attn_Wdt_down': 8.0,
     'L0_attn_Wdt': 8.0,
     'L0_attn_bdt': 8.0,
     'L0_attn_A_log': 8.0,
     'L0_attn_Wout': 8.0,
     'L0_ffn_gate_kernel': 8.0,
     'L0_ffn_w0_kernel': 8.0,
     'L0_ffn_w1_kernel': 8.0,
     'L0_ffn_wo_kernel': 8.0}
    for name, (base, spread) in spreads.items():
        noise = np.random.default_rng([zlib.crc32(name.encode()), seed]).standard_normal(out[name].shape)
        drawn = base * np.exp(spread * noise) if base else spread * noise
        out[name] = jnp.asarray(drawn.astype(out[name].dtype))
    for name, factor in factors.items():
        out[name] = (out[name] * factor).astype(out[name].dtype)
    return out
```

```python
from contextlib import ExitStack

import numpy as np
import concourse.bass as bass
from concourse import mybir

F32 = mybir.dt.float32
BF16 = mybir.dt.bfloat16
U32 = mybir.dt.uint32
I32 = mybir.dt.int32
ALU = mybir.AluOpType
ACT = mybir.ActivationFunctionType
AX = mybir.AxisListType

P = 128
NB = 2
L = 1024
DM = 256
DIN = 512
DXB = 128
DS = 16
DC = 4
NE = 8
MLP = 512
T = NB * L
NT = T // P
NTB = L // P
KD = DM // P
CH = DIN // P
HF = 512
BLK = P // DS
GRP = 64
NBK = GRP // BLK
NG = NB * DIN // GRP
PARTS = 3
KM = MLP // P
LAG = 3
NS = 40
EPS = 1e-5

BX, CB, BDT, DD, BZ, CW, AL = 0, CH, 2 * CH, 3 * CH, 4 * CH, 5 * CH, 5 * CH + CH * DC
NCOL = AL + DIN // BLK
CI8, CI40, CYW, CTRI = P, P + NE, P + NE + NS, P + NE + NS + 2 * P - BLK


def adaln_mamba_moe(nc, x, cols, rows, consts, sels, cT, wmod, wx, wz, wB, wC, wdd, wdt, wout, gate, w0, w1, wo, out):
    ctx = ExitStack()
    with ctx:
        def sb(name, shape, dt=F32):
            return ctx.enter_context(nc.sbuf_tensor(name, shape, dt))

        def sem(name):
            return ctx.enter_context(nc.semaphore(name))

        xs_dram = nc.dram_tensor("expert_in_scratch", (NS * P, DM), F32, kind="Internal").ap()
        ys_dram = nc.dram_tensor("expert_out_scratch", (NS * P, DM), F32, kind="Internal").ap()
        parts_dram = nc.dram_tensor("parts_scratch", (3, PARTS, NB * DIN, L), BF16, kind="Internal").ap()
        partsB_dram = nc.dram_tensor("partsB_scratch", (PARTS, NB * DXB, L), BF16, kind="Internal").ap()

        PS = ctx.enter_context(nc.psum_tensor("PS", [P, 8, HF], F32))

        x_tok = sb("x_tok", [P, NT, DM])
        hT = sb("hT", [P, KD, T])
        uT = sb("uT", [P, NB * CH, L])
        col = sb("col", [P, NCOL])
        bdt2 = sb("bdt2", [P, CH])
        negA = sb("negA", [P, NB, DIN // BLK])
        ident = sb("ident", [P, P])
        iota8 = sb("iota8", [P, NE])
        iota40 = sb("iota40", [P, NS])
        tri_f = sb("tri_f", [P, P])
        ywide = sb("ywide", [P, 2 * P - BLK])
        zrow = sb("zrow", [P, 4 * DM])
        Dcol = sb("Dcol", [P, NB * CH])
        modc = sb("modc", [P, 6 * KD, NB])
        grow = sb("grow", [P, NB, 4, DM])
        row = sb("row", [P, DM])
        gate_sb = sb("gate_sb", [P, KD, NE])
        wz_sb = sb("wz_sb", [P, KD, DIN])
        wout_sb = sb("wout_sb", [P, CH, DM])
        w12 = sb("w12", [P, 4, NT])
        posu = sb("posu", [P, 2, NT], U32)
        etab = sb("etab", [P, NS], I32)
        nhalf = sb("nhalf", [P, NT])
        stat = sb("stat", [P, NT, 6])
        mv = sb("mv", [P, NT, 2])
        rstd = sb("rstd", [P, NT])

        Y = sb("Y", [P, NB * CH * L])
        POOL = 20 * 1024
        pool = sb("pool", [P, POOL])

        def carve(area, size):
            at = [0]

            def take(n, dt=F32):
                words = n if dt is not BF16 else n // 2
                a = area[:, at[0]:at[0] + words]
                at[0] += words
                assert at[0] <= size, at[0]
                return a if dt is F32 else a.bitcast(dt)
            return take

        take = carve(Y, NB * CH * L)
        xn = take(2 * 4 * DM).rearrange("p (r t n) -> p r t n", r=2, t=4)
        xpad = take(2 * (L + 4)).rearrange("p (r n) -> p r n", r=2)
        acc = take(2 * L).rearrange("p (r n) -> p r n", r=2)
        rB = take(L)
        gtmp = acc.rearrange("p r (b n) -> p r b n", b=NB)
        take = carve(pool, POOL)
        wx_sb = take(KD * DIN).rearrange("p (k n) -> p k n", k=KD)
        wB_sb = take(KD * DXB).rearrange("p (k n) -> p k n", k=KD)
        wC_sb = take(KD * DIN).rearrange("p (k n) -> p k n", k=KD)
        wdd_sb = take(KD * DXB).rearrange("p (k n) -> p k n", k=KD)
        wdt_sb = take(DIN)
        cT_sb = take(KD * NB).rearrange("p (k n) -> p k n", k=KD)
        sc = take(KD * NB).rearrange("p (k n) -> p k n", k=KD)
        sc_wide = take(KD * NB * P).rearrange("p (k b n) -> p k b n", k=KD, b=NB)
        dtd = take(L)
        spa = take(L)
        spw = take(L)
        spl = take(L)
        spr = take(L)
        delta = take(L)
        du = take(L)
        r1 = take(2 * L).rearrange("p (r n) -> p r n", r=2)
        parts = take(2 * PARTS * L, BF16).rearrange("p (r a n) -> p r a n", r=2, a=PARTS)
        partsB = take(PARTS * L, BF16).rearrange("p (a n) -> p a n", a=PARTS)
        wmod_sb = pool[:, POOL - KD * 6 * DM:POOL].rearrange("p (k n) -> p k n", k=KD)
        szT = Y[:, :].rearrange("p (g n) -> p g n", n=L)
        take = carve(pool, POOL)
        sels_f = take(7 * P).rearrange("p (s n) -> p s n", s=7)
        sel = take(7 * P, BF16).rearrange("p (s n) -> p s n", s=7)
        stk = take(2 * 3 * 2 * L, BF16).rearrange("p (r k q n) -> p r k q n", r=2, k=3, q=2)
        stB = take(2 * L, BF16).rearrange("p (r n) -> p r n", r=2)
        brep = take(L)
        crep = take(2 * L).rearrange("p (r n) -> p r n", r=2)
        dbu = take(2 * L).rearrange("p (r n) -> p r n", r=2)
        hst = take(2 * L).rearrange("p (r n) -> p r n", r=2)
        prod = take(4 * L).rearrange("p (r n) -> p r n", r=4)
        take = carve(pool, POOL)
        w0_sb = take(NE * KD * MLP).rearrange("p (e k n) -> p e k n", e=NE, k=KD)
        w1_sb = take(NE * KD * MLP).rearrange("p (e k n) -> p e k n", e=NE, k=KD)
        v_st = take(2 * DIN).rearrange("p (r k n) -> p r k n", r=2, k=CH)
        x2n = take(2 * DM).rearrange("p (r n) -> p r n", r=2)
        x2m = take(2 * DM).rearrange("p (r n) -> p r n", r=2)
        h2s = take(2 * KD * P).rearrange("p (r k n) -> p r k n", r=2, k=KD)
        top8 = take(NT * 8).rearrange("p (t n) -> p t n", t=NT)
        idxf = take(NT * 8).rearrange("p (t n) -> p t n", t=NT)
        m8 = take(2 * 8).rearrange("p (r n) -> p r n", r=2)
        i8 = take(2 * 8, U32).rearrange("p (r n) -> p r n", r=2)
        lgt = take(2 * NE).rearrange("p (r n) -> p r n", r=2)
        oh = take(2 * NT * NE).rearrange("p (r t n) -> p r t n", r=2, t=NT)
        take = carve(Y, NB * CH * L)
        ohs = take(NT * NE, BF16)
        tri = take(P, BF16)
        ones = take(P, BF16)
        tots = take(NT * NE).rearrange("p (t n) -> p t n", t=NT)
        pre = take((NT + 1) * NE).rearrange("p (t n) -> p t n", t=NT + 1)
        cnt = take(NE)
        cnti = take(NE, I32)
        off = take(NE + 1)
        offr = take(NE)
        place = take(NT * NE).rearrange("p (t n) -> p t n", t=NT)
        ohp = take(2 * NT * NE).rearrange("p (r t n) -> p r t n", r=2, t=NT)
        posf = take(2 * NT).rearrange("p (r t) -> p r t", r=2)
        ef = take(NS)
        h2row = hT[:, :, :].rearrange("p k n -> p (k n)").rearrange("p (t n) -> p t n", t=NT)
        wo_sb = Y[:, :].rearrange("p (e k n) -> p e k n", e=NE, k=KM)
        take = carve(uT[:, :, :].rearrange("p c n -> p (c n)"), NB * CH * L)
        xg = take(2 * DM).rearrange("p (r n) -> p r n", r=2)
        xgT = take(2 * KD * P).rearrange("p (r k n) -> p r k n", r=2, k=KD)
        sil = take(2 * MLP).rearrange("p (r n) -> p r n", r=2)
        inter = take(2 * MLP).rearrange("p (r n) -> p r n", r=2)
        intT = take(2 * MLP).rearrange("p (r k n) -> p r k n", r=2, k=KM)
        yo = take(2 * DM).rearrange("p (r n) -> p r n", r=2)
        back_rows = pool[:, 0:2 * NT * DM].rearrange("p (r t n) -> p r t n", r=2, t=NT)

        x_in, small_in, w_in, sels_in = sem("x_in"), sem("small_in"), sem("w_in"), sem("sels_in")
        silu_c, c_wide, mod_mm, mod_step = sem("silu_c"), sem("c_wide"), sem("mod_mm"), sem("mod_step")
        col_done, zero_done, nhalf_done = sem("col_done"), sem("zero_done"), sem("nhalf_done")
        stat_done, aggr_done, rstd_done = sem("stat_done"), sem("aggr_done"), sem("rstd_done")
        xn_done, turned, h_done = sem("xn_done"), sem("turned"), sem("h_done")
        dtd_mm, dtd_copied, b_mm, x_mm, c_mm, dt_mm = (sem(n) for n in ("dtd_mm", "dtd_copied", "b_mm", "x_mm", "c_mm", "dt_mm"))
        xpad_done, u_done, conv_step = sem("xpad_done"), sem("u_done"), sem("conv_step")
        sp_abs, sp_exp, sp_w, sp_ln, sp_k, sp_l = (sem(n) for n in ("sp_abs", "sp_exp", "sp_w", "sp_ln", "sp_k", "sp_l"))
        dt_free, delta_done, du_done = sem("dt_free"), sem("delta_done"), sem("du_done")
        hi_done, r1_done, mid_done, lo_done, cps_free = (sem(n) for n in ("hi_done", "r1_done", "mid_done", "lo_done", "cps_free"))
        bhi_done, br1_done, bmid_done, blo_done, partsB_out = (sem(n) for n in ("bhi_done", "br1_done", "bmid_done", "blo_done", "partsB_out"))
        parts_out = [sem("parts_out0"), sem("parts_out1")]
        a_over, b_over, c_over, passed = sem("a_over"), sem("b_over"), sem("c_over"), sem("passed")
        sel_done, stk_free, cr_mm, cr_copied = sem("sel_done"), sem("stk_free"), sem("cr_mm"), sem("cr_copied")
        stk_in = [sem("stk_in0"), sem("stk_in1")]
        dl_mm, du_mm, exp_done, dbu_done = sem("dl_mm"), sem("du_mm"), sem("exp_done"), sem("dbu_done")
        scan_done, prod_done, ysum_done, yev_done = sem("scan_done"), sem("prod_done"), sem("ysum_done"), sem("yev_done")
        d_done, zero_rows, xs_zeroed, z_mm, sz_done = (sem(n) for n in ("d_done", "zero_rows", "xs_zeroed", "z_mm", "sz_done"))
        c_step, o_mm, h2_mm, g_mm, rs_step, h2_done = (
            sem(n) for n in ("c_step", "o_mm", "h2_mm", "g_mm", "rs_step", "h2_done"))
        route_step, count_mm, ex_done = sem("route_step"), sem("count_mm"), sem("ex_done")
        w01_in, wo_in, sent, xg_in = sem("w01_in"), sem("wo_in"), sem("sent"), [sem("xg_in0"), sem("xg_in1")]
        xT_mm, xT_done, h01_mm, sil_done, inter_done = (sem(n) for n in ("xT_mm", "xT_done", "h01_mm", "sil_done", "inter_done"))
        iT_mm, iT_done, oe_mm, yo_done = (sem(n) for n in ("iT_mm", "iT_done", "oe_mm", "yo_done"))
        yo_out = [sem("yo_out0"), sem("yo_out1")]
        placed, weighed, fin_done, out_done = sem("placed"), sem("weighed"), sem("fin_done"), sem("out_done")
        got = [sem(f"got{q}") for q in range(4)]

        ITEMS = 3 * CH
        CUSE = 2 + 2 * (GRP // DS)

        def pair(bank):
            return PS[:, bank:bank + 2, :].rearrange("p a n -> p (a n)")

        ROUTE = dict(gap=3, picked=6)

        STEPS = ("v", "ob", "og", "x2", "st", "ag", "xn", "lg", "mx", "mi", "km", "ki")

        def stepped(name, j, it):
            return it * (2 * len(STEPS)) + (2 * STEPS.index(name) + j + 1)

        x_dram = x.rearrange("(t p) n -> p t n", p=P)
        out_dram = out.rearrange("(t p) n -> p t n", p=P)

        block = ctx.enter_context(nc.Block())

        @block.sync
        def _(sp):
            sp.dma_start(x_tok[:, :, :], x_dram).then_inc(x_in, 16)
            sp.dma_start(cT_sb, cT.rearrange("(k p) n -> p k n", p=P)).then_inc(small_in, 16)
            sp.dma_start(wmod_sb, wmod.rearrange("(k p) n -> p k n", p=P)).then_inc(small_in, 16)
            sp.dma_start(ident[:, :], consts[:, 0:P]).then_inc(small_in, 16)
            sp.dma_start(iota8[:, :], consts[:, CI8:CI8 + NE]).then_inc(small_in, 16)
            sp.dma_start(iota40[:, :], consts[:, CI40:CI40 + NS]).then_inc(small_in, 16)
            sp.dma_start(ywide[:, :], consts[:, CYW:CYW + 2 * P - BLK]).then_inc(small_in, 16)
            sp.dma_start(tri_f[:, :], consts[:, CTRI:CTRI + P]).then_inc(small_in, 16)
            sp.dma_start(col[:, :], cols).then_inc(small_in, 16)
            for dst, src in ((wdd_sb, wdd), (wx_sb, wx), (wB_sb, wB), (wC_sb, wC), (wz_sb[:, :, :], wz),
                             (wout_sb[:, :, :], wout), (gate_sb[:, :, :], gate)):
                sp.dma_start(dst, src.rearrange("(k p) n -> p k n", p=P)).then_inc(w_in, 16)
            sp.dma_start(wdt_sb, wdt).then_inc(w_in, 16)
            sp.dma_start(row[:, :], rows).then_inc(w_in, 16)

            sp.wait_ge(zero_rows, 1)
            for i in range(NS // 4):
                sp.dma_start(xs_dram[4 * P * i:4 * P * i + 4 * P, :].rearrange("(n p) c -> p n c", p=P),
                             zrow[:, :].rearrange("p (n c) -> p n c", c=DM)).then_inc(xs_zeroed, 16)

            sp.sem_inc(parts_out[0], 16)
            sp.sem_inc(parts_out[1], 16)
            sp.sem_inc(partsB_out, 16)
            with sp.Fori(0, NB) as b:
                sp.wait_ge(blo_done, b + 1)
                sp.dma_start(partsB_dram[:, bass.ds(b * DXB, P), :].rearrange("a p n -> p a n"),
                             partsB).then_inc(partsB_out, 16)
                for i in range(ITEMS):
                    c, kind = i // 3, i % 3
                    sp.wait_ge(lo_done, b * ITEMS + (i + 1))
                    sp.dma_start(parts_dram[kind, :, bass.ds(b * DIN + c * P, P), :].rearrange("a p n -> p a n"),
                                 parts[:, i % 2]).then_inc(parts_out[i % 2], 16)
            for landed, n in ((partsB_out, NB), (parts_out[0], NB * ITEMS // 2), (parts_out[1], NB * ITEMS // 2)):
                sp.wait_ge(landed, 16 * (1 + n))

            sp.wait_ge(a_over, 4)
            sp.dma_start(sels_f[0:96], sels.rearrange("p (s n) -> p s n", s=7)).then_inc(sels_in, 16)
            sp.sem_inc(stk_free, 2)
            with sp.Fori(0, NG // 2) as g2:
                for r in range(2):
                    g = g2 * 2 + r
                    sp.wait_ge(stk_free, g2 * 2 + (r + 1))
                    for kind in range(3):
                        for q in range(2):
                            for a in range(PARTS):
                                sp.dma_start(stk[32 * a:32 * a + 32, r, kind, q, :],
                                             parts_dram[kind, a, bass.ds(g * GRP + 32 * q, 32), :]).then_inc(stk_in[r], 16)
                    for a in range(PARTS):
                        sp.dma_start(stB[DS * a:DS * a + DS, r, :],
                                     partsB_dram[a, bass.ds(g * DS, DS), :]).then_inc(stk_in[r], 16)

            sp.wait_ge(b_over, 4)
            for dst, src in ((w0_sb, w0), (w1_sb, w1)):
                for e in range(NE):
                    sp.dma_start(dst[:, e], src[e].rearrange("(k p) n -> p k n", p=P)).then_inc(w01_in, 16)
            sp.wait_ge(c_over, 4)
            for e in range(NE):
                sp.dma_start(wo_sb[:, e], wo[e].rearrange("(k p) n -> p k n", p=P)).then_inc(wo_in, 16)
            sp.wait_ge(sent, 16 * 2 * NT)

            def rows_in(slot, r):
                sp.dma_start(xg[:, r, :], xs_dram[bass.ds(slot * P, P), :]).then_inc(xg_in[r], 16)

            def rows_out(slot, r):
                sp.wait_ge(yo_done, slot + 3)
                sp.dma_start(ys_dram[bass.ds(slot * P, P), :], yo[:, r, :]).then_inc(yo_out[r], 16)

            rows_in(0, 0)
            rows_in(1, 1)
            with sp.Fori(0, NS // 2 - 1) as s2:
                for r in range(2):
                    sp.wait_ge(xT_mm, s2 * 2 + (r + 1))
                    rows_in(s2 * 2 + (r + 2), r)
                for r in range(2):
                    rows_out(s2 * 2 + r, r)
            for r in range(2):
                rows_out(NS - 2 + r, r)
            with sp.Fori(0, NT // 4) as t4:
                sp.wait_ge(fin_done, t4 * 4 + 4)
                sp.dma_start(out_dram[:, bass.ds(t4 * 4, 4), :], x_tok[:, bass.ds(t4 * 4, 4), :]).then_inc(out_done, 16)
            sp.wait_ge(out_done, 16 * (NT // 4))
        @block.tensor
        def _(pe):
            pe.wait_ge(silu_c, 1)
            pe.wait_ge(c_wide, KD * NB)
            for j in range(6 * KD):
                for k in range(KD):
                    m = pe.matmul(PS[:, 0, NB * j:NB * j + NB], wmod_sb[:, k, P * j:P * j + P], sc[:, k, :],
                                  start=k == 0, stop=k == KD - 1)
            for b in range(NB):
                for i, which in enumerate((2, 5, 4, 3)):
                    for k in range(KD):
                        m = pe.matmul(PS[:, 1 + 2 * b + i // 2, DM * (i % 2):DM * (i % 2) + DM], sc_wide[:, k, b, :],
                                      wmod_sb[:, k, DM * which:DM * which + DM], start=k == 0, stop=k == KD - 1)
            m.then_inc(mod_mm, 1)

            pe.wait_ge(mod_step, 4)
            pe.sem_inc(h_done, 4)
            with pe.Fori(0, NB) as b:
                for j in range(2):
                    pe.wait_ge(xn_done, b * 8 + (4 * j + 4))
                    pe.wait_ge(h_done, b * 4 + (2 * j + 2))
                    for k in range(KD):
                        for t in range(4):
                            m = pe.transpose(PS[:, 4 + 2 * j + k, P * t:P * t + P], xn[:, j, t, P * k:P * k + P], ident[:, :])
                    m.then_inc(turned, 1)

            pe.wait_ge(w_in, 16 * 9)
            pe.wait_ge(h_done, 4 + 2 * 4)
            pe.sem_inc(cps_free, CH)
            pe.sem_inc(dt_free, 1)
            pe.sem_inc(br1_done, 1)
            with pe.Fori(0, NB) as b:
                def project(bank, k_chunks, w, rhs, done):
                    for half in range(2):
                        for k in range(k_chunks):
                            m = pe.matmul(PS[:, bank + half, :], w(k), rhs(k, half), start=k == 0, stop=k == k_chunks - 1)
                    m.then_inc(done, 1)

                def h_cols(k, half):
                    return hT[:, k, bass.ds(b * L + half * HF, HF)]

                pe.wait_ge(br1_done, b + 1)
                project(6, KD, lambda k: wdd_sb[:, k, :], h_cols, dtd_mm)
                for c in range(CH):
                    if c < 2:
                        pe.wait_ge(cps_free, b * CH + (c + 3))
                    else:
                        pe.wait_ge(xpad_done, b * CH + (c - 1))
                    project(2 * (c % 2), KD, lambda k: wx_sb[:, k, P * c:P * c + P], h_cols, x_mm)
                    if c == 1:
                        pe.wait_ge(dtd_copied, b + 1)
                        project(6, KD, lambda k: wB_sb[:, k, :], h_cols, b_mm)
                for c in range(CH):
                    if c < 2:
                        pe.wait_ge(xpad_done, b * CH + (c + 3))
                    else:
                        pe.wait_ge(cps_free, b * CH + (c - 1 + CH))
                    project(2 * (c % 2), KD, lambda k: wC_sb[:, k, P * c:P * c + P], h_cols, c_mm)
                    pe.wait_ge(dt_free, b * CH + (c + 1))
                    project(4, 1, lambda k: wdt_sb[:, P * c:P * c + P],
                            lambda k, half: dtd[:, HF * half:HF * half + HF], dt_mm)
            pe.wait_ge(cps_free, CH + NB * CH)
            pe.sem_inc(sz_done, 2)
            with pe.Fori(0, NB) as b:
                for c in range(CH):
                    pe.wait_ge(sz_done, b * CH + (c + 1))
                    project(2 * (c % 2), KD, lambda k: wz_sb[:, k, P * c:P * c + P],
                            lambda k, half: hT[:, k, bass.ds(b * L + half * HF, HF)], z_mm)
            pe.drain().then_inc(a_over, 1)

            pe.wait_ge(sel_done, 1)
            pe.wait_ge(a_over, 4)
            pe.sem_inc(scan_done, 2)
            pe.sem_inc(dbu_done, 2)
            pe.sem_inc(yev_done, 1)

            def front(g2, r, k):
                q, j = k // 4, k % 4

                def n(per, extra):
                    return g2 * (2 * per) + (r * per + extra)

                if k == 0:
                    pe.wait_ge(stk_in[r], g2 * (16 * 21) + 16 * 21)
                    for half in range(2):
                        pe.wait_ge(dbu_done, n(2 * NBK, half + 1))
                        pe.matmul(PS[:, 4 + half, :], sel[0:48, 6, :], stB[0:48, r, HF * half:HF * half + HF],
                                  start=True, stop=True).then_inc(cr_mm, 1)
                for half in range(2):
                    if k == 0:
                        pe.wait_ge(cr_copied, n(CUSE, half + 1))
                    elif k % 2:
                        pe.wait_ge(cr_copied, n(CUSE, k + half + 2))
                    else:
                        pe.wait_ge(dbu_done, n(2 * NBK, 2 * k + half + 1))
                    pe.matmul(PS[:, 4 + half, :], sel[0:96, j, :], stk[0:96, r, 2, q, HF * half:HF * half + HF],
                              start=True, stop=True).then_inc(du_mm, 1)
                pe.wait_ge(scan_done, n(NBK, k + 1))
                for half in range(2):
                    m = pe.matmul(PS[:, 2 * (k % 2) + half, :], sel[0:96, j, :],
                                  stk[0:96, r, 1, q, HF * half:HF * half + HF], start=True, stop=True)
                m.then_inc(dl_mm, 1)
                if k % 2 == 0:
                    for half in range(2):
                        pe.wait_ge(dbu_done, n(2 * NBK, 2 * k + half + 3))
                        pe.matmul(PS[:, 4 + half, :], sel[0:96, 4 + j // 2, :], stk[0:96, r, 0, q, HF * half:HF * half + HF],
                                  start=True, stop=True).then_inc(cr_mm, 1)
                if k == NBK - 1:
                    pe.wait_ge(dl_mm, n(NBK, k + 1))
                    pe.sem_inc(stk_free, 1)

            def back(g2, r, k):
                j = r * NBK + k
                if j == 0:
                    pe.wait_ge(yev_done, g2 + 1)
                pe.wait_ge(prod_done, g2 * (2 * NBK) + (j + 1 + 4))
                for half in range(2):
                    m = pe.matmul(PS[:, 6 + half, :], ywide[:, P - BLK - BLK * j:2 * P - BLK - BLK * j],
                                  prod[:, k % 4, HF * half:HF * half + HF], start=j == 0, stop=j == 2 * NBK - 1)
                m.then_inc(ysum_done, 1)

            for k in range(LAG):
                front(0, 0, k)
            with pe.Fori(0, NG // 2 - 1) as g2:
                for r in range(2):
                    for k in range(NBK):
                        if k + LAG < NBK:
                            front(g2, r, k + LAG)
                        else:
                            front(g2 + r, 1 - r, k + LAG - NBK)
                        back(g2, r, k)
            for r in range(2):
                for k in range(NBK):
                    if k + LAG < NBK:
                        front(NG // 2 - 1, r, k + LAG)
                    elif r == 0:
                        front(NG // 2 - 1, 1, k + LAG - NBK)
                    back(NG // 2 - 1, r, k)
            pe.drain().then_inc(b_over, 1)

            pe.wait_ge(b_over, 4)
            with pe.Fori(0, NT // 2) as it:
                for j in range(2):
                    pe.wait_ge(c_step, stepped("v", j, it))
                    for k in range(CH):
                        m = pe.matmul(PS[:, j, 0:DM], v_st[:, j, k, :], wout_sb[:, k, :], start=k == 0, stop=k == CH - 1)
                    m.then_inc(o_mm, 1)
                for j in range(2):
                    pe.wait_ge(rs_step, it * 10 + (3 * j + 6))
                    for k in range(KD):
                        m = pe.transpose(PS[:, 2 + j, P * k:P * k + P], x2m[:, j, P * k:P * k + P], ident[:, :])
                    m.then_inc(h2_mm, 1)
                for j in range(2):
                    pe.wait_ge(h2_done, it * 2 + (j + 1))
                    for k in range(KD):
                        m = pe.matmul(PS[:, 4 + j, 0:NE], h2s[:, j, k, :], gate_sb[:, k, :], start=k == 0, stop=k == KD - 1)
                    m.then_inc(g_mm, 1)
            pe.wait_ge(route_step, ROUTE["picked"])
            pe.matmul(PS[:, 6, 0:NT * NE], tri, ohs, start=True, stop=True)
            pe.matmul(PS[:, 7, 0:NT * NE], ones, ohs, start=True, stop=True).then_inc(count_mm, 1)
            pe.drain().then_inc(c_over, 1)

            def turn(s2, r):
                pe.wait_ge(xg_in[r], s2 * 16 + 16)
                pe.wait_ge(xT_done, s2 * 2 + (r + 1))
                for k in range(KD):
                    m = pe.transpose(PS[:, 0, P * k:P * k + P], xg[:, r, P * k:P * k + P], ident[:, :])
                m.then_inc(xT_mm, 1)

            def expert_of(s2, r):
                return pe.value_load(etab[0:1, bass.ds(s2 * 2 + r, 1)], min_val=0, max_val=NE - 1)

            def hidden(s2, r):
                e = expert_of(s2, r)
                pe.wait_ge(xT_done, s2 * 2 + (r + 2))
                pe.wait_ge(inter_done, s2 * 2 + (r + 1))
                for bank, w in ((2 + 2 * r, w0_sb), (3 + 2 * r, w1_sb)):
                    for k in range(KD):
                        m = pe.matmul(PS[:, bank, :], xgT[:, r, k, :],
                                      w[:, bass.ds(e, 1), k, :].rearrange("p e n -> p (e n)"), start=k == 0, stop=k == KD - 1)
                m.then_inc(h01_mm, 1)

            def turn_inter(s2, r):
                pe.wait_ge(inter_done, s2 * 2 + (r + 3))
                pe.wait_ge(iT_done, s2 * 2 + (r + 1))
                for k in range(KM):
                    m = pe.transpose(PS[:, 1, P * k:P * k + P], inter[:, r, P * k:P * k + P], ident[:, :])
                m.then_inc(iT_mm, 1)

            def outward(s2, r):
                e = expert_of(s2, r)
                pe.wait_ge(iT_done, s2 * 2 + (r + 2))
                pe.wait_ge(yo_done, s2 * 2 + (r + 1))
                for k in range(KM):
                    m = pe.matmul(PS[:, 6 + r, 0:DM], intT[:, r, k, :],
                                  wo_sb[:, bass.ds(e, 1), k, :].rearrange("p e n -> p (e n)"), start=k == 0, stop=k == KM - 1)
                m.then_inc(oe_mm, 1)

            pe.wait_ge(c_over, 4)
            pe.wait_ge(w01_in, 16 * 2 * NE)
            pe.wait_ge(wo_in, 16 * NE)
            pe.sem_inc(xT_done, 1)
            pe.sem_inc(inter_done, 2)
            pe.sem_inc(iT_done, 1)
            pe.sem_inc(yo_done, 2)
            turn(0, 0)
            turn(0, 1)
            hidden(0, 0)
            with pe.Fori(0, NS // 2 - 1) as s2:
                for r in range(2):
                    turn(s2 + 1, r)
                    turn_inter(s2, r)
                    hidden(s2 + r, 1 - r)
                    outward(s2, r)
            last = NS // 2 - 1
            turn_inter(last, 0)
            hidden(last, 1)
            outward(last, 0)
            turn_inter(last, 1)
            outward(last, 1)

        @block.scalar
        def _(act):
            act.wait_ge(small_in, 16 * 8)
            act.activation(sc, cT_sb, ACT.Silu).then_inc(silu_c, 1)
            for b in range(NB):
                act.activation(negA[:, b, :], col[:, AL:NCOL], ACT.Exp).then_inc(col_done, 1)

            act.wait_ge(mod_step, 3)
            with act.Fori(0, NB) as b:
                for j in range(2):
                    act.wait_ge(turned, b * 2 + (j + 1 + 2))
                    for k in range(KD):
                        act.activation(hT[:, k, bass.ds(b * L + j * HF, HF)], PS[:, 4 + 2 * j + k, :], ACT.Identity,
                                       bias=modc[:, k, bass.ds(b, 1)], scale=modc[:, KD + k, bass.ds(b, 1)]).then_inc(h_done, 1)

            act.wait_ge(zero_done, 2)
            with act.Fori(0, NB) as b:
                def padded(c):
                    act.wait_ge(x_mm, b * CH + (c + 1))
                    act.activation(xpad[:, c % 2, DC - 1:DC - 1 + L], pair(2 * (c % 2)), ACT.Identity,
                                   bias=col[:, BX + c:BX + c + 1]).then_inc(xpad_done, 1)

                def silu_u(c):
                    act.wait_ge(conv_step, b * (CH * DC) + (c + 1) * DC)
                    act.activation(uT[:, bass.ds(b * CH + c, 1), :], acc[:, c % 2:c % 2 + 1, :], ACT.Silu,
                                   bias=col[:, CB + c:CB + c + 1]).then_inc(u_done, 1)

                def hi(i, src):
                    act.wait_ge(parts_out[i % 2], b * (16 * (ITEMS // 2)) + 16 * (i // 2 + 1))
                    act.activation(parts[:, i % 2, 0, :], src, ACT.Copy).then_inc(hi_done, 1)

                def mid(i):
                    act.wait_ge(r1_done, b * ITEMS + (i + 1 + 1))
                    act.activation(parts[:, i % 2, 1, :], r1[:, i % 2, :], ACT.Copy).then_inc(mid_done, 1)

                act.wait_ge(dtd_mm, b + 1)
                act.activation(dtd, pair(6), ACT.Copy).then_inc(dtd_copied, 1)
                padded(0)
                padded(1)
                silu_u(0)
                padded(2)
                silu_u(1)
                padded(3)
                act.wait_ge(b_mm, b + 1)
                act.wait_ge(partsB_out, b * 16 + 16)
                act.activation(partsB[:, 0, :], pair(6), ACT.Copy).then_inc(bhi_done, 1)
                silu_u(2)
                silu_u(3)
                act.wait_ge(br1_done, b + 2)
                act.activation(partsB[:, 1, :], rB, ACT.Copy).then_inc(bmid_done, 1)
                for c in range(CH):
                    act.wait_ge(c_mm, b * CH + (c + 1))
                    hi(3 * c, pair(2 * (c % 2)))
                    act.wait_ge(dt_mm, b * CH + (c + 1))
                    act.activation(spa, pair(4), ACT.Abs, bias=bdt2[:, c:c + 1]).then_inc(sp_abs, 1)
                    act.wait_ge(sp_abs, b * CH + (c + 1))
                    act.activation(spa, spa, ACT.Exp, scale=-1.0).then_inc(sp_exp, 1)
                    mid(3 * c)
                    act.wait_ge(sp_w, b * CH + (c + 1))
                    act.activation(spl, spw, ACT.Ln).then_inc(sp_ln, 1)
                    act.wait_ge(delta_done, b * CH + (c + 1))
                    hi(3 * c + 1, delta)
                    mid(3 * c + 1)
                    act.wait_ge(du_done, b * CH + (c + 1))
                    hi(3 * c + 2, du)
                    mid(3 * c + 2)
            with act.Fori(0, NB) as b:
                for c in range(CH):
                    act.wait_ge(z_mm, b * CH + (c + 1))
                    act.activation(szT[:, bass.ds(b * CH + c, 1), :], pair(2 * (c % 2)), ACT.Silu,
                                   bias=col[:, BZ + c:BZ + c + 1]).then_inc(sz_done, 1)
            act.drain().then_inc(a_over, 1)

            act.wait_ge(a_over, 4)
            act.wait_ge(sels_in, 16)
            act.activation(sel[0:96], sels_f[0:96], ACT.Copy).then_inc(sel_done, 1)
            act.sem_inc(prod_done, 4)
            act.sem_inc(ysum_done, 4)
            decay = negA[:, :, :].rearrange("p b n -> p (b n)")

            def front(g2, r, k):
                def n(per, extra):
                    return g2 * (2 * per) + (r * per + extra)

                def copy_half(dst, use, half):
                    act.wait_ge(cr_mm, n(CUSE, use + half + 1))
                    act.activation(dst[:, HF * half:HF * half + HF], PS[:, 4 + half, :], ACT.Copy).then_inc(cr_copied, 1)

                if k == 0:
                    act.wait_ge(dbu_done, n(2 * NBK, 2))
                    copy_half(brep, 0, 0)
                    copy_half(brep, 0, 1)
                act.wait_ge(dl_mm, n(NBK, k + 1))
                act.activation(pair(2 * (k % 2)), pair(2 * (k % 2)), ACT.Exp,
                               scale=decay[:, bass.ds(n(NBK, k), 1)]).then_inc(exp_done, 1)
                if k % 2 == 0:
                    act.wait_ge(prod_done, n(NBK, k + 2))
                    copy_half(crep[:, k // 2 % 2, :], 2 + k, 0)
                    copy_half(crep[:, k // 2 % 2, :], 2 + k, 1)

            with act.Fori(0, NG // 2) as g2:
                for r in range(2):
                    for k in range(NBK):
                        front(g2, r, k)
            act.drain().then_inc(b_over, 1)

            act.wait_ge(b_over, 4)
            with act.Fori(0, NT // 2) as it:
                for j in range(2):
                    act.wait_ge(h2_mm, it * 2 + (j + 1))
                    act.activation(h2s[:, j], PS[:, 2 + j, 0:DM].rearrange("p (k n) -> p k n", k=KD), ACT.Copy).then_inc(h2_done, 1)
            act.wait_ge(route_step, ROUTE["gap"])
            act.activation(w12[:, 1, :], w12[:, 0, :], ACT.Exp).then_inc(ex_done, 1)
            act.drain().then_inc(c_over, 1)

            def take_rows(s2, r):
                act.wait_ge(xT_mm, s2 * 2 + (r + 1))
                act.wait_ge(h01_mm, s2 * 2 + (r + 1))
                act.activation(xgT[:, r], PS[:, 0, 0:DM].rearrange("p (k n) -> p k n", k=KD),
                               ACT.Copy).then_inc(xT_done, 1)

            def silu_h(s2, r):
                act.wait_ge(h01_mm, s2 * 2 + (r + 3))
                act.wait_ge(inter_done, s2 * 2 + (r + 1))
                act.activation(sil[:, r, :], PS[:, 2 + 2 * r, :], ACT.Silu).then_inc(sil_done, 1)

            def leave(s2, r):
                act.wait_ge(oe_mm, s2 * 2 + (r + 3))
                act.wait_ge(yo_out[r], s2 * 16 + 16)
                act.activation(yo[:, r, :], PS[:, 6 + r, 0:DM], ACT.Copy).then_inc(yo_done, 1)

            act.wait_ge(c_over, 4)
            act.sem_inc(h01_mm, 2)
            for r in range(2):
                act.sem_inc(yo_out[r], 16)
            take_rows(0, 0)
            take_rows(0, 1)
            silu_h(0, 0)
            with act.Fori(0, NS // 2 - 1) as s2:
                for r in range(2):
                    take_rows(s2 + 1, r)
                    silu_h(s2 + r, 1 - r)
                    leave(s2, r)
            last = NS // 2 - 1
            silu_h(last, 1)
            leave(last, 0)
            leave(last, 1)

        @block.vector
        def _(dve):
            dve.wait_ge(small_in, 16 * 8)
            dve.wait_ge(silu_c, 1)
            for k in range(KD):
                for b in range(NB):
                    dve.tensor_scalar(sc_wide[:, k, b, :], ident[:, :], 0.0, sc[:, k, b:b + 1], ALU.mult, ALU.add).then_inc(c_wide, 1)
            dve.memset(zrow[:, :], 0.0).then_inc(zero_rows, 1)
            for b in range(NB):
                dve.tensor_copy(Dcol[:, CH * b:CH * b + CH], col[:, DD:DD + CH]).then_inc(d_done, 1)
            dve.memset(xpad[:, :, 0:DC - 1], 0.0).then_inc(zero_done, 1)
            dve.tensor_scalar(bdt2[:, :], col[:, BDT:BDT + CH], 2.0, None, ALU.mult).then_inc(zero_done, 1)

            dve.wait_ge(col_done, NB)
            dve.tensor_scalar(negA[:, :, :], negA[:, :, :], -1.0, None, ALU.mult).then_inc(col_done, 1)

            dve.wait_ge(x_in, 16)
            with dve.Fori(0, NT) as t:
                dve.bn_stats(stat[:, bass.ds(t, 1), :], x_tok[:, bass.ds(t, 1), :]).then_inc(stat_done, 1)
            dve.wait_ge(stat_done, NT)
            for t in range(NT):
                dve.bn_aggr(mv[:, t, :], stat[:, t, :]).then_inc(aggr_done, 1)

            dve.wait_ge(mod_mm, 1)
            dve.tensor_copy(modc[:, :, :], PS[:, 0, 0:6 * KD * NB].rearrange("p (j b) -> p j b", b=NB)).then_inc(mod_step, 1)
            dve.wait_ge(mod_step, 1)
            for n, j in ((1, KD), (2, 4 * KD)):
                dve.tensor_scalar(modc[:, j:j + KD, :], modc[:, j:j + KD, :], 1.0, None, ALU.add).then_inc(mod_step, 1)
            dve.tensor_copy(grow[:, :, :, :].rearrange("p b i n -> p (b i n)"),
                            PS[:, 1:5, :].rearrange("p a n -> p (a n)")).then_inc(mod_step, 1)
            dve.wait_ge(mod_step, 4)
            gates = grow[:, :, 0:2, :].rearrange("p b i n -> p b (i n)")
            dve.tensor_scalar(grow[:, :, 2, :], grow[:, :, 2, :], 1.0, None, ALU.add).then_inc(mod_step, 1)
            dve.tensor_scalar(gtmp[:, 0], gates, 0.0, 2.0, ALU.is_ge, ALU.mult).then_inc(mod_step, 1)
            dve.scalar_tensor_tensor(gtmp[:, 1], gates, -1.0, gates, ALU.mult, ALU.max).then_inc(mod_step, 1)
            dve.wait_ge(mod_step, 7)
            dve.tensor_scalar(gtmp[:, 1], gtmp[:, 1], 0.25, None, ALU.max).then_inc(mod_step, 1)
            dve.wait_ge(mod_step, 8)
            dve.scalar_tensor_tensor(gates, gtmp[:, 0], -1.0, gtmp[:, 1], ALU.add, ALU.mult).then_inc(mod_step, 1)

            dve.wait_ge(rstd_done, 2)
            dve.sem_inc(turned, 2)
            with dve.Fori(0, NB) as b:
                for j in range(2):
                    dve.wait_ge(turned, b * 2 + (j + 1))
                    for t in range(4):
                        at = b * NTB + (4 * j + t)
                        dve.tensor_scalar(xn[:, j, t:t + 1, :], x_tok[:, bass.ds(at, 1), :], mv[:, bass.ds(at, 1), 0],
                                          rstd[:, bass.ds(at, 1)], ALU.subtract, ALU.mult).then_inc(xn_done, 1)

            dve.sem_inc(u_done, 2)
            dve.sem_inc(r1_done, 1)
            with dve.Fori(0, NB) as b:
                for c in range(CH):
                    dve.wait_ge(xpad_done, b * CH + (c + 1))
                    dve.wait_ge(u_done, b * CH + (c + 1))
                    for k in range(DC):
                        tap = col[:, CW + DC * c + k:CW + DC * c + k + 1]
                        if k == 0:
                            dve.tensor_scalar(acc[:, c % 2, :], xpad[:, c % 2, k:k + L], tap, None, ALU.mult).then_inc(conv_step, 1)
                        else:
                            dve.wait_ge(conv_step, b * (CH * DC) + (c * DC + k))
                            dve.scalar_tensor_tensor(acc[:, c % 2, :], xpad[:, c % 2, k:k + L], tap, acc[:, c % 2, :],
                                                     ALU.mult, ALU.add).then_inc(conv_step, 1)
                dve.wait_ge(bhi_done, b + 1)
                dve.tensor_tensor(rB, pair(6), partsB[:, 0, :], ALU.subtract).then_inc(br1_done, 1)
                dve.wait_ge(bmid_done, b + 1)
                dve.wait_ge(br1_done, b + 2)
                dve.tensor_tensor(partsB[:, 2, :], rB, partsB[:, 1, :], ALU.subtract).then_inc(blo_done, 1)

                def rest(i, src):
                    dve.wait_ge(hi_done, b * ITEMS + (i + 1))
                    return dve.tensor_tensor(r1[:, i % 2, :], src, parts[:, i % 2, 0, :], ALU.subtract).then_inc(r1_done, 1)

                def low(i):
                    dve.wait_ge(mid_done, b * ITEMS + (i + 1))
                    dve.tensor_tensor(parts[:, i % 2, 2, :], r1[:, i % 2, :], parts[:, i % 2, 1, :], ALU.subtract).then_inc(lo_done, 1)

                for c in range(CH):
                    at = b * CH + (c + 1)
                    rest(3 * c, pair(2 * (c % 2)))
                    dve.wait_ge(r1_done, b * ITEMS + (3 * c + 2))
                    dve.sem_inc(cps_free, 1)
                    dve.wait_ge(sp_exp, at)
                    dve.tensor_scalar(spw, spa, 1.0, None, ALU.add).then_inc(sp_w, 1)
                    low(3 * c)
                    dve.wait_ge(sp_ln, at)
                    dve.scalar_tensor_tensor(spw, spw, -1.0, spa, ALU.add, ALU.subtract).then_inc(sp_k, 1)
                    dve.tensor_scalar(spr, pair(4), bdt2[:, c:c + 1], 0.0, ALU.add, ALU.max).then_inc(dt_free, 1)
                    dve.wait_ge(sp_k, at)
                    dve.tensor_tensor(spl, spl, spw, ALU.subtract).then_inc(sp_l, 1)
                    dve.wait_ge(sp_l, b * (2 * CH) + (2 * c + 1))
                    dve.tensor_tensor(spl, spl, spa, ALU.min).then_inc(sp_l, 1)
                    dve.wait_ge(sp_l, b * (2 * CH) + (2 * c + 2))
                    dve.wait_ge(dt_free, at + 1)
                    dve.tensor_tensor(delta, spl, spr, ALU.add).then_inc(delta_done, 1)
                    rest(3 * c + 1, delta)
                    low(3 * c + 1)
                    rest(3 * c + 2, du)
                    low(3 * c + 2)
            dve.drain().then_inc(a_over, 1)

            dve.wait_ge(a_over, 4)

            def drive(g2, r, k):
                dve.wait_ge(scan_done, g2 * (2 * NBK) + (r * NBK + k + 1))
                for half in range(2):
                    cols_of = slice(HF * half, HF * half + HF)
                    if k == 0:
                        dve.wait_ge(cr_copied, g2 * (2 * CUSE) + (r * CUSE + half + 1))
                    dve.wait_ge(du_mm, g2 * (4 * NBK) + (2 * (r * NBK + k) + half + 1))
                    dve.tensor_tensor(dbu[:, k % 2, cols_of], PS[:, 4 + half, :], brep[:, cols_of], ALU.mult).then_inc(dbu_done, 1)

            def scan(g2, r, k):
                n = r * NBK + k
                dve.wait_ge(exp_done, g2 * (2 * NBK) + (n + 1))
                dve.wait_ge(dbu_done, g2 * (4 * NBK) + (2 * n + 2 + 2))
                dve.wait_ge(prod_done, g2 * (2 * NBK) + (n + 3))
                dve.tensor_tensor_scan(hst[:, k % 2, :], pair(2 * (k % 2)), dbu[:, k % 2, :], 0.0,
                                       ALU.mult, ALU.add).then_inc(scan_done, 1)

            def leave(g2):
                dve.wait_ge(ysum_done, g2 * (2 * NBK) + (2 * NBK + 4))
                chunk = uT[:, bass.ds(g2, 1), :].rearrange("p c n -> p (c n)")
                dve.scalar_tensor_tensor(chunk, chunk, Dcol[:, bass.ds(g2, 1)], pair(6), ALU.mult, ALU.add).then_inc(yev_done, 1)

            def chunk_of_blocks(g2, first):
                for r in range(2):
                    drive(g2, r, 0)
                    for k in range(1, NBK):
                        drive(g2, r, k)
                        scan(g2, r, k - 1)
                        if r == 0 and k == LAG and not first:
                            leave(g2 - 1)
                    scan(g2, r, NBK - 1)

            chunk_of_blocks(0, True)
            with dve.Fori(1, NG // 2) as g2:
                chunk_of_blocks(g2, False)
            leave(NG // 2 - 1)
            dve.drain().then_inc(b_over, 1)

            dve.wait_ge(b_over, 4)
            y4 = uT[:, :, :].rearrange("p (b c) n -> p b c n", b=NB)
            sz4 = szT.rearrange("p (b c) n -> p b c n", b=NB)
            with dve.Fori(0, NB) as b:
                with dve.Fori(0, NTB // 2) as t:
                    it = b * (NTB // 2) + t

                    def done(name, j):
                        dve.wait_ge(c_step, stepped(name, j, it))

                    def rows_of(j):
                        return x_tok[:, bass.ds(b * NTB + t * 2 + j, 1), :]

                    def tokens(a, j):
                        return a[:, bass.ds(b, 1), :, bass.ds(t * (2 * P) + j * P, P)].rearrange("p b c n -> p (b c) n")

                    for j in range(2):
                        dve.tensor_tensor(v_st[:, j], tokens(y4, j), tokens(sz4, j), ALU.mult).then_inc(c_step, 1)
                    for j in range(2):
                        dve.wait_ge(o_mm, it * 2 + (j + 1))
                        dve.tensor_tensor(x2n[:, j, :], PS[:, j, 0:DM], row[:, :], ALU.add).then_inc(c_step, 1)
                    for j in range(2):
                        done("ob", j)
                        dve.tensor_tensor(x2n[:, j:j + 1, :], x2n[:, j:j + 1, :], grow[:, bass.ds(b, 1), 0, :], ALU.mult).then_inc(c_step, 1)
                    for j in range(2):
                        done("og", j)
                        dve.tensor_tensor(rows_of(j), rows_of(j), x2n[:, j:j + 1, :], ALU.add).then_inc(c_step, 1)
                    for j in range(2):
                        done("x2", j)
                        dve.sem_inc(passed, 1)
                        dve.bn_stats(stat[:, j, :], rows_of(j)).then_inc(c_step, 1)
                    for j in range(2):
                        done("st", j)
                        dve.sem_inc(passed, 1)
                        dve.bn_aggr(mv[:, j, :], stat[:, j, :]).then_inc(c_step, 1)
                    for j in range(2):
                        dve.wait_ge(rs_step, it * 10 + (2 * j + 2))
                        dve.tensor_scalar(x2n[:, j:j + 1, :], rows_of(j), mv[:, j, 0:1], rstd[:, j:j + 1],
                                          ALU.subtract, ALU.mult).then_inc(c_step, 1)
                    for j in range(2):
                        dve.wait_ge(g_mm, it * 2 + (j + 1))
                        dve.tensor_copy(lgt[:, j, :], PS[:, 4 + j, 0:NE]).then_inc(c_step, 1)
                    for j in range(2):
                        done("lg", j)
                        dve.sem_inc(passed, 1)
                        dve.max(m8[:, j, :], lgt[:, j, :]).then_inc(c_step, 1)
                    for j in range(2):
                        done("mx", j)
                        dve.sem_inc(passed, 1)
                        dve.max_index(i8[:, j, :], m8[:, j, :], lgt[:, j, :]).then_inc(c_step, 1)
                    for j in range(2):
                        dve.tensor_copy(top8[:, bass.ds(b * NTB + t * 2 + j, 1), :], m8[:, j:j + 1, :]).then_inc(c_step, 1)
                    for j in range(2):
                        done("mi", j)
                        dve.tensor_copy(idxf[:, bass.ds(b * NTB + t * 2 + j, 1), :], i8[:, j:j + 1, :]).then_inc(c_step, 1)

            route = [0]

            def step(ins):
                ins.then_inc(route_step, 1)
                route[0] += 1

            def settled():
                dve.wait_ge(route_step, route[0])

            dve.wait_ge(c_step, stepped("ki", 1, NT // 2 - 1))
            step(dve.tensor_copy(tri, tri_f[:, :]))
            step(dve.memset(ones, 1.0))
            step(dve.tensor_tensor(w12[:, 0, :], top8[:, :, 1], top8[:, :, 0], ALU.subtract))
            assert route[0] == ROUTE["gap"]
            for i in range(2):
                step(dve.tensor_tensor(oh[:, i], iota8[:, :].unsqueeze(1).broadcast_to([P, NT, NE]),
                                       idxf[:, :, i:i + 1].broadcast_to([P, NT, NE]), ALU.is_equal))
            settled()
            step(dve.tensor_tensor(ohs, oh[:, 0].rearrange("p t n -> p (t n)"), oh[:, 1].rearrange("p t n -> p (t n)"), ALU.add))
            assert route[0] == ROUTE["picked"]
            dve.wait_ge(count_mm, 1)
            step(dve.tensor_copy(tots.rearrange("p t n -> p (t n)"), PS[:, 7, 0:NT * NE]))
            step(dve.memset(pre[:, 0, :], 0.0))
            for t in range(NT):
                settled()
                step(dve.tensor_tensor(pre[:, t + 1, :], pre[:, t, :], tots[:, t, :], ALU.add))
            settled()
            step(dve.tensor_scalar(cnti, pre[:, NT, :], float(P - 1), None, ALU.add))
            settled()
            step(dve.tensor_scalar(cnti, cnti, 7, None, ALU.arith_shift_right))
            settled()
            step(dve.tensor_copy(cnt, cnti))
            step(dve.memset(off[:, 0:1], 0.0))
            for e in range(NE - 1):
                settled()
                step(dve.tensor_tensor(off[:, e + 1:e + 2], off[:, e:e + 1], cnt[:, e:e + 1], ALU.add))
            settled()
            step(dve.tensor_scalar(offr, off[:, 0:NE], float(P), None, ALU.mult))
            step(dve.tensor_scalar(ef, iota40[:, :], off[:, 1:2], None, ALU.is_ge))
            step(dve.tensor_tensor(place, PS[:, 6, 0:NT * NE].rearrange("p (t n) -> p t n", n=NE), pre[:, 0:NT, :], ALU.add))
            for e in range(2, NE):
                settled()
                step(dve.scalar_tensor_tensor(ef, iota40[:, :], off[:, e:e + 1], ef, ALU.is_ge, ALU.add))
            settled()
            step(dve.tensor_copy(etab[:, :], ef))
            step(dve.tensor_tensor(place, place, offr.unsqueeze(1).broadcast_to([P, NT, NE]), ALU.add))
            settled()
            for i in range(2):
                step(dve.tensor_tensor(ohp[:, i], oh[:, i], place, ALU.mult))
            settled()
            for i in range(2):
                step(dve.tensor_reduce(posf[:, i, :], ohp[:, i], AX.X, ALU.add))
            settled()
            step(dve.tensor_copy(posu[:, :, :], posf))
            settled()
            dve.sem_inc(placed, 1)
            dve.wait_ge(ex_done, 1)
            step(dve.tensor_scalar(w12[:, 2, :], w12[:, 1, :], 1.0, None, ALU.add))
            settled()
            step(dve.reciprocal(w12[:, 2, :], w12[:, 2, :]))
            settled()
            step(dve.tensor_tensor(w12[:, 3, :], w12[:, 1, :], w12[:, 2, :], ALU.mult))
            settled()
            dve.drain().then_inc(c_over, 1)

            def gate_h(s2, r):
                dve.wait_ge(sil_done, s2 * 2 + (r + 1))
                dve.wait_ge(iT_mm, s2 * 2 + (r + 1))
                dve.tensor_tensor(inter[:, r, :], sil[:, r, :], PS[:, 3 + 2 * r, :], ALU.mult).then_inc(inter_done, 1)

            def take_inter(s2, r):
                dve.wait_ge(iT_mm, s2 * 2 + (r + 3))
                dve.wait_ge(oe_mm, s2 * 2 + (r + 1))
                dve.tensor_copy(intT[:, r].rearrange("p k n -> p (k n)"), PS[:, 1, :]).then_inc(iT_done, 1)

            dve.wait_ge(c_over, 4)
            dve.sem_inc(iT_mm, 2)
            dve.sem_inc(oe_mm, 2)
            gate_h(0, 0)
            with dve.Fori(0, NS // 2 - 1) as s2:
                for r in range(2):
                    take_inter(s2, r)
                    gate_h(s2 + r, 1 - r)
            last = NS // 2 - 1
            take_inter(last, 0)
            gate_h(last, 1)
            take_inter(last, 1)

            for q in range(4):
                t4 = slice(4 * q, 4 * q + 4)
                b = q // 2
                dve.wait_ge(got[q], 16 * 8)
                step(dve.tensor_tensor(back_rows[:, 0, t4, :], back_rows[:, 0, t4, :],
                                       w12[:, 2, t4].unsqueeze(2).broadcast_to([P, 4, DM]), ALU.mult))
                settled()
                dve.wait_ge(weighed, q + 1)
                step(dve.tensor_tensor(back_rows[:, 0, t4, :], back_rows[:, 0, t4, :], back_rows[:, 1, t4, :], ALU.add))
                settled()
                step(dve.tensor_tensor(back_rows[:, 0, t4, :], back_rows[:, 0, t4, :],
                                       grow[:, b, 1:2, :].broadcast_to([P, 4, DM]), ALU.mult))
                settled()
                dve.tensor_tensor(x_tok[:, t4, :], x_tok[:, t4, :], back_rows[:, 0, t4, :], ALU.add).then_inc(fin_done, 4)

        @block.gpsimd
        def _(gp):
            gp.memset(nhalf[:, :], -0.5).then_inc(nhalf_done, 1)
            gp.wait_ge(nhalf_done, 1)
            gp.wait_ge(aggr_done, NT)
            gp.tensor_scalar(rstd[:, :], mv[:, :, 1], EPS, None, ALU.add).then_inc(rstd_done, 1)
            gp.wait_ge(rstd_done, 1)
            gp.tensor_tensor(rstd[:, :], rstd[:, :], nhalf[:, :], ALU.pow).then_inc(rstd_done, 1)

            with gp.Fori(0, NB) as b:
                for c in range(CH):
                    gp.wait_ge(delta_done, b * CH + (c + 1))
                    gp.wait_ge(u_done, b * CH + (c + 3))
                    gp.wait_ge(r1_done, b * ITEMS + (3 * c + 1))
                    gp.tensor_tensor(du, delta, uT[:, bass.ds(b * CH + c, 1), :].rearrange("p c n -> p (c n)"), ALU.mult).then_inc(du_done, 1)
            gp.drain().then_inc(a_over, 1)

            gp.wait_ge(a_over, 4)
            with gp.Fori(0, NG) as g:
                for k in range(NBK):
                    gp.wait_ge(scan_done, g * NBK + (k + 3))
                    if k % 2 == 0:
                        gp.wait_ge(cr_copied, g * CUSE + (2 + k + 2))
                    gp.wait_ge(ysum_done, g * NBK + (k + 1))
                    gp.tensor_tensor(prod[:, k % 4, :], hst[:, k % 2, :], crep[:, k // 2 % 2, :], ALU.mult).then_inc(prod_done, 1)
            gp.drain().then_inc(b_over, 1)

            gp.wait_ge(b_over, 4)
            with gp.Fori(0, NB) as b:
                with gp.Fori(0, NTB // 2) as t:
                    it = b * (NTB // 2) + t
                    for j in range(2):
                        gp.wait_ge(c_step, stepped("ag", j, it))
                        gp.sem_inc(passed, 1)
                        gp.tensor_scalar(rstd[:, j:j + 1], mv[:, j, 1:2], EPS, None, ALU.add).then_inc(rs_step, 1)
                        gp.wait_ge(rs_step, it * 10 + (2 * j + 1))
                        gp.tensor_tensor(rstd[:, j:j + 1], rstd[:, j:j + 1], nhalf[:, 0:1], ALU.pow).then_inc(rs_step, 1)
                    for j in range(2):
                        row_j = slice(j, j + 1)
                        gp.wait_ge(c_step, stepped("xn", j, it))
                        gp.sem_inc(passed, 1)
                        gp.tensor_tensor(x2n[:, row_j, :], x2n[:, row_j, :], grow[:, bass.ds(b, 1), 2, :], ALU.mult).then_inc(rs_step, 1)
                        gp.wait_ge(rs_step, it * 10 + (3 * j + 5))
                        gp.sem_inc(passed, 1)
                        gp.tensor_tensor(x2m[:, row_j, :], x2n[:, row_j, :], grow[:, bass.ds(b, 1), 3, :], ALU.add).then_inc(rs_step, 1)
                        gp.wait_ge(rs_step, it * 10 + (3 * j + 6))
                        gp.sem_inc(passed, 1)
                        gp.tensor_copy(h2row[:, bass.ds(b * NTB + t * 2 + j, 1), :], x2m[:, row_j, :]).then_inc(rs_step, 1)
            gp.wait_ge(rs_step, 10 * (NT // 2))
            gp.drain().then_inc(c_over, 1)

            gp.wait_ge(placed, 1)
            gp.wait_ge(xs_zeroed, 16 * NS // 4)
            for t in range(NT):
                for i in range(2):
                    gp.indirect_dma_start(out=xs_dram, out_offset=bass.IndirectOffsetOnAxis(ap=posu[:, i, t:t + 1], axis=0),
                                          in_=h2row[:, t, :], in_offset=None).then_inc(sent, 16)
            gp.wait_ge(yo_out[0], 16 + 16 * (NS // 2))
            gp.wait_ge(yo_out[1], 16 + 16 * (NS // 2))
            for t in range(NT):
                for i in range(2):
                    gp.indirect_dma_start(out=back_rows[:, i, t, :], out_offset=None, in_=ys_dram,
                                          in_offset=bass.IndirectOffsetOnAxis(ap=posu[:, i, t:t + 1], axis=0)
                                          ).then_inc(got[t // 4], 16)
            for q in range(4):
                t4 = slice(4 * q, 4 * q + 4)
                gp.wait_ge(got[q], 16 * 8)
                gp.tensor_tensor(back_rows[:, 1, t4, :], back_rows[:, 1, t4, :],
                                 w12[:, 3, t4].unsqueeze(2).broadcast_to([P, 4, DM]), ALU.mult).then_inc(weighed, 1)


def kernel(**inputs):
    import numpy as _np
    import concourse.bacc as _bacc
    from concourse import mybir as _mybir
    from concourse.bass_utils import run_bass_kernel_spmd as _run

    a = {k[3:]: _np.asarray(v) for k, v in inputs.items()}
    at = {k.replace("attn_", ""): v for k, v in a.items()}

    def by_channel(v):
        v = v.reshape(CH, P, -1)
        return v.transpose(1, 0, 2).reshape(P, -1)

    def repeated(v):
        v = v.reshape(DXB // DS, 1, DS, -1)
        return _np.broadcast_to(v, (DXB // DS, DIN // DXB, DS, v.shape[-1])).reshape(DIN, -1)

    cols = _np.concatenate([by_channel(repeated(at["bx"])), by_channel(at["conv_b"]), by_channel(at["bdt"]),
                            by_channel(at["D"]), by_channel(at["bz"]), by_channel(at["conv_w"].reshape(DIN, DC)),
                            at["A_log"].reshape(DIN // BLK, P).T], axis=1)
    rows = _np.broadcast_to(at["bout"][None], (P, DM))

    consts = _np.zeros((P, CTRI + P), _np.float32)
    consts[:, :P] = _np.eye(P)
    consts[:, CI8:CI8 + NE] = _np.arange(NE)
    consts[:, CI40:CI40 + NS] = _np.arange(NS)
    consts[_np.arange(P), CYW + P - BLK + _np.arange(P) // DS] = 1
    consts[:, CTRI:] = _np.triu(_np.ones((P, P)), 1)
    sels = _np.zeros((96, 7, P), _np.float32)
    m = _np.arange(P)
    for part in range(PARTS):
        for j in range(4):
            sels[32 * part + 8 * j + m // DS, j, m] = 1
        for h in range(2):
            sels[32 * part + DS * h + m % DS, 4 + h, m] = 1
        sels[DS * part + m % DS, 6, m] = 1

    arrays = {
        "x": at["hidden_states"].reshape(T, DM), "cols": cols, "rows": rows, "consts": consts, "sels": sels.reshape(96, -1),
        "cT": a["c"].T, "wmod": a["wmod"], "wx": repeated(at["Wx"]).T, "wz": at["Wz"].T, "wB": at["WB"].T, "wC": at["WC"].T,
        "wdd": at["Wdt_down"].T, "wdt": at["Wdt"].T, "wout": at["Wout"].T, "gate": a["ffn_gate_kernel"],
        "w0": a["ffn_w0_kernel"], "w1": a["ffn_w1_kernel"], "wo": a["ffn_wo_kernel"],
    }
    nc = _bacc.Bacc("TRN2", target_bir_lowering=False, num_devices=1)
    args, feeds = [], {}
    for name, v in arrays.items():
        v = _np.ascontiguousarray(v)
        feeds[f"in_{name}"] = v
        args.append(nc.dram_tensor(f"in_{name}", v.shape, _mybir.dt.from_np(v.dtype), kind="ExternalInput").ap())
    args.append(nc.dram_tensor("out", (T, DM), _mybir.dt.float32, kind="ExternalOutput").ap())
    adaln_mamba_moe(nc, *args)
    r = _run(nc, [feeds], core_ids=[0])
    return r.results[0]["out"].reshape(NB, L, DM)
```

```python
from contextlib import ExitStack

import numpy as np
import concourse.bass as bass
from concourse import mybir

F32 = mybir.dt.float32
BF16 = mybir.dt.bfloat16
U32 = mybir.dt.uint32
I32 = mybir.dt.int32
ALU = mybir.AluOpType
ACT = mybir.ActivationFunctionType
AX = mybir.AxisListType

P = 128
NB = 2
L = 1024
DM = 256
DIN = 512
DXB = 128
DS = 16
DC = 4
NE = 8
MLP = 512
T = NB * L
NT = T // P
NTB = L // P
KD = DM // P
CH = DIN // P
HF = 512
BLK = P // DS
GRP = 64
NBK = GRP // BLK
NG = NB * DIN // GRP
PARTS = 3
KM = MLP // P
LAG = 3
NS = (2 * T - NE) // P + NE
EPS = 1e-5

BX, CB, BDT, DD, BZ, CW, AL = 0, CH, 2 * CH, 3 * CH, 4 * CH, 5 * CH, 5 * CH + CH * DC
NCOL = AL + DIN // BLK
CI8, CIS, CYW, CTRI = P, P + NE, P + NE + NS, P + NE + NS + 2 * P - BLK
SPAIRS = (NS - 3) // 2
ZS = 3
assert NS % 2 and NS % ZS == 0


def adaln_mamba_moe(nc, x, cols, rows, consts, sels, cT, wmod, wx, wz, wB, wC, wdd, wdt, wout, gate, w0, w1, wo, out):
    ctx = ExitStack()
    with ctx:
        def sb(name, shape, dt=F32):
            return ctx.enter_context(nc.sbuf_tensor(name, shape, dt))

        def sem(name):
            return ctx.enter_context(nc.semaphore(name))

        xs_dram = nc.dram_tensor("expert_in_scratch", (NS * P, DM), F32, kind="Internal").ap()
        ys_dram = nc.dram_tensor("expert_out_scratch", (NS * P, DM), F32, kind="Internal").ap()
        parts_dram = nc.dram_tensor("parts_scratch", (2, NB * DIN // 32, PARTS, 32, L), BF16, kind="Internal").ap()
        C_dram = nc.dram_tensor("C_scratch", (NB * DIN, L), F32, kind="Internal").ap()
        B_dram = nc.dram_tensor("B_scratch", (NB * DXB, L), F32, kind="Internal").ap()

        PS = ctx.enter_context(nc.psum_tensor("PS", [P, 8, HF], F32))

        x_tok = sb("x_tok", [P, NT, DM])
        hT = sb("hT", [P, KD, T])
        uT = sb("uT", [P, NB * CH, L])
        col = sb("col", [P, NCOL])
        bdt2 = sb("bdt2", [P, CH])
        negA = sb("negA", [P, NB, DIN // BLK])
        ident = sb("ident", [P, P])
        iota8 = sb("iota8", [P, NE])
        iota_s = sb("iota_s", [P, NS])
        tri_f = sb("tri_f", [P, P])
        ywide = sb("ywide", [P, 2 * P - BLK])
        zrow = sb("zrow", [P, ZS * DM])
        Dcol = sb("Dcol", [P, NB * CH])
        modc = sb("modc", [P, 6 * KD, NB])
        grow = sb("grow", [P, NB, 4, DM])
        row = sb("row", [P, DM])
        gate_sb = sb("gate_sb", [P, KD, NE])
        wz_sb = sb("wz_sb", [P, KD, DIN])
        wout_sb = sb("wout_sb", [P, CH, DM])
        w12 = sb("w12", [P, 4, NT])
        posu = sb("posu", [P, 2, NT], U32)
        etab = sb("etab", [P, NS], I32)
        nhalf = sb("nhalf", [P, NT])
        stat = sb("stat", [P, NT, 6])
        mv = sb("mv", [P, NT, 2])
        rstd = sb("rstd", [P, NT])

        Y = sb("Y", [P, NB * CH * L])
        POOL = 20 * 1024
        pool = sb("pool", [P, POOL])

        def carve(area, size):
            at = [0]

            def take(n, dt=F32):
                words = n if dt is not BF16 else n // 2
                a = area[:, at[0]:at[0] + words]
                at[0] += words
                assert at[0] <= size, at[0]
                return a if dt is F32 else a.bitcast(dt)
            return take

        take = carve(Y, NB * CH * L)
        xn = take(2 * 4 * DM).rearrange("p (r t n) -> p r t n", r=2, t=4)
        C_st = Y[:, 0:2 * L].rearrange("p (r n) -> p r n", r=2)
        B_st = take(L)
        xpad = take(2 * (L + 4)).rearrange("p (r n) -> p r n", r=2)
        acc = take(2 * L).rearrange("p (r n) -> p r n", r=2)
        cT_sb = take(KD * NB).rearrange("p (k n) -> p k n", k=KD)
        sc = take(KD * NB).rearrange("p (k n) -> p k n", k=KD)
        sc_wide = take(KD * NB * P).rearrange("p (k b n) -> p k b n", k=KD, b=NB)
        gate_tmp = acc.rearrange("p r (b n) -> p r b n", b=NB)
        take = carve(pool, POOL)
        wx_sb = take(KD * DIN).rearrange("p (k n) -> p k n", k=KD)
        wB_sb = take(KD * DXB).rearrange("p (k n) -> p k n", k=KD)
        wC_sb = take(KD * DIN).rearrange("p (k n) -> p k n", k=KD)
        wdd_sb = take(KD * DXB).rearrange("p (k n) -> p k n", k=KD)
        wdt_sb = take(DIN)
        dtd = take(L)
        spa = take(2 * L).rearrange("p (r n) -> p r n", r=2)
        spw = take(2 * L).rearrange("p (r n) -> p r n", r=2)
        spl = take(2 * L).rearrange("p (r n) -> p r n", r=2)
        delta = take(2 * L).rearrange("p (r n) -> p r n", r=2)
        r1 = take(2 * L).rearrange("p (r n) -> p r n", r=2)
        parts = take(4 * PARTS * L, BF16).rearrange("p (r a n) -> p r a n", r=4, a=PARTS)
        wmod_sb = pool[:, POOL - KD * 6 * DM:POOL].rearrange("p (k n) -> p k n", k=KD)
        szT = Y[:, :].rearrange("p (g n) -> p g n", n=L)
        take = carve(pool, POOL)
        sels_f = take(4 * P).rearrange("p (s n) -> p s n", s=4)
        sel = take(4 * P, BF16).rearrange("p (s n) -> p s n", s=4)
        stk = take(2 * 2 * 2 * L, BF16).rearrange("p (r k q n) -> p r k q n", r=2, k=2, q=2)
        brep = take(2 * L).rearrange("p (r n) -> p r n", r=2)
        crep = take(4 * L).rearrange("p (r n) -> p r n", r=4)
        dbu = take(2 * L).rearrange("p (r n) -> p r n", r=2)
        hst = take(2 * L).rearrange("p (r n) -> p r n", r=2)
        prod = take(4 * L).rearrange("p (r n) -> p r n", r=4)
        da = hT[:, 0, :].rearrange("p (r n) -> p r n", r=2)
        take = carve(pool, POOL)
        w0_sb = take(NE * KD * MLP).rearrange("p (e k n) -> p e k n", e=NE, k=KD)
        w1_sb = take(NE * KD * MLP).rearrange("p (e k n) -> p e k n", e=NE, k=KD)
        v_st = take(2 * DIN).rearrange("p (r k n) -> p r k n", r=2, k=CH)
        x2n = take(2 * DM).rearrange("p (r n) -> p r n", r=2)
        x2m = take(2 * DM).rearrange("p (r n) -> p r n", r=2)
        h2s = take(2 * KD * P).rearrange("p (r k n) -> p r k n", r=2, k=KD)
        top8 = take(NT * 8).rearrange("p (t n) -> p t n", t=NT)
        idxf = take(NT * 8).rearrange("p (t n) -> p t n", t=NT)
        i8 = take(NT * 8, U32).rearrange("p (t n) -> p t n", t=NT)
        lgt = take(NT * NE).rearrange("p (t n) -> p t n", t=NT)
        oh = take(2 * NT * NE).rearrange("p (r t n) -> p r t n", r=2, t=NT)
        take = carve(Y, NB * CH * L)
        ohs = take(NT * NE, BF16)
        tri = take(P, BF16)
        ones = take(P, BF16)
        tots = take(NT * NE).rearrange("p (t n) -> p t n", t=NT)
        pre = take((NT + 1) * NE).rearrange("p (t n) -> p t n", t=NT + 1)
        cnt = take(NE)
        cnti = take(NE, I32)
        off = take(NE + 1)
        offr = take(NE)
        place = take(NT * NE).rearrange("p (t n) -> p t n", t=NT)
        ohp = take(2 * NT * NE).rearrange("p (r t n) -> p r t n", r=2, t=NT)
        posf = take(2 * NT).rearrange("p (r t) -> p r t", r=2)
        ef = take(NS)
        h2row = hT[:, :, :].rearrange("p k n -> p (k n)").rearrange("p (t n) -> p t n", t=NT)
        wo_sb = Y[:, :].rearrange("p (e k n) -> p e k n", e=NE, k=KM)
        take = carve(uT[:, :, :].rearrange("p c n -> p (c n)"), NB * CH * L)
        xg = take(2 * DM).rearrange("p (r n) -> p r n", r=2)
        xgT = take(2 * KD * P).rearrange("p (r k n) -> p r k n", r=2, k=KD)
        sil = take(2 * MLP).rearrange("p (r n) -> p r n", r=2)
        inter = take(2 * MLP).rearrange("p (r n) -> p r n", r=2)
        intT = take(2 * MLP).rearrange("p (r k n) -> p r k n", r=2, k=KM)
        yo = take(2 * DM).rearrange("p (r n) -> p r n", r=2)
        back_rows = pool[:, 0:2 * NT * DM].rearrange("p (r t n) -> p r t n", r=2, t=NT)

        x_in, small_in, w_in, sels_in = sem("x_in"), sem("small_in"), sem("w_in"), sem("sels_in")
        silu_c, c_wide, mod_mm, mod_step = sem("silu_c"), sem("c_wide"), sem("mod_mm"), sem("mod_step")
        col_done, zero_done, nhalf_done = sem("col_done"), sem("zero_done"), sem("nhalf_done")
        stat_done, aggr_done, rstd_done = sem("stat_done"), sem("aggr_done"), sem("rstd_done")
        xn_done, turned, h_done = sem("xn_done"), sem("turned"), sem("h_done")
        six_mm, six_copied, x_mm, dt_mm = (sem(n) for n in ("six_mm", "six_copied", "x_mm", "dt_mm"))
        xpad_done, u_done, conv_step = sem("xpad_done"), sem("u_done"), sem("conv_step")
        sp_abs, sp_exp, sp_w, sp_ln, sp_k, sp_sub, sp_min = (
            sem(n) for n in ("sp_abs", "sp_exp", "sp_w", "sp_ln", "sp_k", "sp_sub", "sp_min"))
        dt_free, delta_done, du_done = sem("dt_free"), sem("delta_done"), sem("du_done")
        hi_done, r1_done, mid_done, lo_done = (sem(n) for n in ("hi_done", "r1_done", "mid_done", "lo_done"))
        parts_out = [sem(f"parts_out{r}") for r in range(4)]
        B_out, C_out = sem("B_out"), [sem("C_out0"), sem("C_out1")]
        a_over, b_over, c_over, passed = sem("a_over"), sem("b_over"), sem("c_over"), sem("passed")
        sel_done, stk_free = sem("sel_done"), sem("stk_free")
        stk_in, brep_in = [sem("stk_in0"), sem("stk_in1")], [sem("brep_in0"), sem("brep_in1")]
        crep_in = [sem(f"crep_in{h}") for h in range(4)]
        dl_mm, du_mm, exp_done, dbu_done = sem("dl_mm"), sem("du_mm"), sem("exp_done"), sem("dbu_done")
        scan_done, prod_done, ysum_done, yev_done = sem("scan_done"), sem("prod_done"), sem("ysum_done"), sem("yev_done")
        d_done, zero_rows, xs_zeroed, z_mm, sz_done = (sem(n) for n in ("d_done", "zero_rows", "xs_zeroed", "z_mm", "sz_done"))
        v_done, o_mm, x2_step, aggr2_done, rstd2_done = (
            sem(n) for n in ("v_done", "o_mm", "x2_step", "aggr2_done", "rstd2_done"))
        m_step, kept, h2_mm, h2_done, g_mm = (sem(n) for n in ("m_step", "kept", "h2_mm", "h2_done", "g_mm"))
        route_step, count_mm, ex_done, max_done, index_done = (
            sem(n) for n in ("route_step", "count_mm", "ex_done", "max_done", "index_done"))
        w01_in, wo_in, sent, xg_in = sem("w01_in"), sem("wo_in"), sem("sent"), [sem("xg_in0"), sem("xg_in1")]
        xT_mm, xT_done, h0_mm, h01_mm, sil_done, inter_done = (sem(n) for n in ("xT_mm", "xT_done", "h0_mm", "h01_mm", "sil_done", "inter_done"))
        iT_mm, iT_done, oe_mm, yo_done = (sem(n) for n in ("iT_mm", "iT_done", "oe_mm", "yo_done"))
        yo_out = [sem("yo_out0"), sem("yo_out1")]
        placed, weighed, fin_done, out_done = sem("placed"), sem("weighed"), sem("fin_done"), sem("out_done")
        got = [sem(f"got{q}") for q in range(NT // 2)]

        ITEMS = 2 * CH
        SIX = 2 + CH

        def pair(bank):
            return PS[:, bank:bank + 2, :].rearrange("p a n -> p (a n)")

        ROUTE = dict(gap=5, picked=8)

        x_dram = x.rearrange("(t p) n -> p t n", p=P)
        out_dram = out.rearrange("(t p) n -> p t n", p=P)

        block = ctx.enter_context(nc.Block())

        @block.sync
        def _(sp):
            sp.dma_start(x_tok[:, :, :], x_dram).then_inc(x_in, 16)
            sp.dma_start(cT_sb, cT.rearrange("(k p) n -> p k n", p=P)).then_inc(small_in, 16)
            sp.dma_start(wmod_sb, wmod.rearrange("(k p) n -> p k n", p=P)).then_inc(small_in, 16)
            sp.dma_start(ident[:, :], consts[:, 0:P]).then_inc(small_in, 16)
            sp.dma_start(iota8[:, :], consts[:, CI8:CI8 + NE]).then_inc(small_in, 16)
            sp.dma_start(iota_s[:, :], consts[:, CIS:CIS + NS]).then_inc(small_in, 16)
            sp.dma_start(ywide[:, :], consts[:, CYW:CYW + 2 * P - BLK]).then_inc(small_in, 16)
            sp.dma_start(tri_f[:, :], consts[:, CTRI:CTRI + P]).then_inc(small_in, 16)
            sp.dma_start(col[:, :], cols).then_inc(small_in, 16)
            for dst, src in ((wdd_sb, wdd), (wx_sb, wx), (wB_sb, wB), (wC_sb, wC), (wz_sb[:, :, :], wz),
                             (wout_sb[:, :, :], wout), (gate_sb[:, :, :], gate)):
                sp.dma_start(dst, src.rearrange("(k p) n -> p k n", p=P)).then_inc(w_in, 16)
            sp.dma_start(wdt_sb, wdt).then_inc(w_in, 16)
            sp.dma_start(row[:, :], rows).then_inc(w_in, 16)

            sp.wait_ge(zero_rows, 1)
            for i in range(NS // ZS):
                sp.dma_start(xs_dram[ZS * P * i:ZS * P * i + ZS * P, :].rearrange("(n p) c -> p n c", p=P),
                             zrow[:, :].rearrange("p (n c) -> p n c", c=DM)).then_inc(xs_zeroed, 16)

            for r in range(4):
                sp.sem_inc(parts_out[r], 64)
            for r in range(2):
                sp.sem_inc(C_out[r], 16)
            sp.sem_inc(B_out, 16)
            with sp.Fori(0, NB) as b:
                def C_to_dram(c):
                    sp.wait_ge(six_copied, b * SIX + (2 + c + 2))
                    sp.dma_start(C_dram[bass.ds(b * DIN + c * P, P), :], C_st[:, c % 2, :]).then_inc(C_out[c % 2], 16)

                sp.wait_ge(six_copied, b * SIX + 3)
                sp.dma_start(B_dram[bass.ds(b * DXB, P), :], B_st).then_inc(B_out, 16)
                C_to_dram(0)
                for i in range(ITEMS):
                    if i == ITEMS // 2:
                        C_to_dram(1)
                        C_to_dram(2)
                        C_to_dram(3)
                    c, kind = i // 2, i % 2
                    sp.wait_ge(lo_done, b * ITEMS + (i + 1 + 2))
                    for q in range(4):
                        sp.dma_start(parts_dram[kind, bass.ds(b * (4 * CH) + c * 4 + q, 1)].rearrange("o a c n -> c (o a) n"),
                                     parts[32 * q:32 * q + 32, i % 4]).then_inc(parts_out[i % 4], 16)
            for landed, n in [(B_out, NB)] + [(o, NB * CH // 2) for o in C_out] + [(o, NB * ITEMS) for o in parts_out]:
                first = 4 if landed in parts_out else 1
                sp.wait_ge(landed, 16 * (first + n))

            sp.wait_ge(a_over, 4)
            sp.dma_start(sels_f[0:96], sels.rearrange("p (s n) -> p s n", s=4)).then_inc(sels_in, 16)
            sp.sem_inc(stk_free, 2)
            sp.sem_inc(ysum_done, 2 * NBK)
            with sp.Fori(0, NG // 2) as g2:
                for r in range(2):
                    g = g2 * 2 + r
                    sp.wait_ge(stk_free, g2 * 2 + (r + 1))
                    for kind in range(2):
                        for q in range(2):
                            sp.dma_start(stk[0:96, r, kind, q, :],
                                         parts_dram[kind, bass.ds(g * 2 + q, 1)].rearrange("o a c n -> (o a c) n")
                                         ).then_inc(stk_in[r], 16)
                    sp.wait_ge(ysum_done, g2 * (2 * NBK) + (r * NBK + NBK))
                    sp.dma_start(brep[:, r, :], B_dram[bass.ds(g * DS, DS), :].unsqueeze(1).broadcast_to([DS, BLK, L])
                                 ).then_inc(brep_in[r], 16)
                    for h in range(4):
                        sp.wait_ge(ysum_done, g2 * (2 * NBK) + (r * NBK + 2 * h + 2 + NBK))
                        sp.dma_start(crep[:, h, :],
                                     C_dram[bass.ds(g * GRP + h * DS, DS), :].unsqueeze(1).broadcast_to([DS, BLK, L])
                                     ).then_inc(crep_in[h], 16)

            sp.wait_ge(b_over, 4)
            for dst, src in ((w0_sb, w0), (w1_sb, w1)):
                for e in range(NE):
                    sp.dma_start(dst[:, e], src[e].rearrange("(k p) n -> p k n", p=P)).then_inc(w01_in, 16)
            sp.wait_ge(c_over, 4)
            for e in range(NE):
                sp.dma_start(wo_sb[:, e], wo[e].rearrange("(k p) n -> p k n", p=P)).then_inc(wo_in, 16)
            sp.wait_ge(sent, 16 * 2 * NT)

            def rows_in(slot, r):
                sp.dma_start(xg[:, r, :], xs_dram[bass.ds(slot * P, P), :]).then_inc(xg_in[r], 16)

            rows_in(0, 0)
            rows_in(1, 1)
            with sp.Fori(0, SPAIRS) as s2:
                for r in range(2):
                    sp.wait_ge(xT_mm, s2 * 2 + (r + 1))
                    rows_in(s2 * 2 + (r + 2), r)
            sp.wait_ge(xT_mm, NS - 2)
            rows_in(NS - 1, 0)
            with sp.Fori(0, NT // 2) as t2:
                sp.wait_ge(fin_done, t2 * 2 + 2)
                sp.dma_start(out_dram[:, bass.ds(t2 * 2, 2), :], x_tok[:, bass.ds(t2 * 2, 2), :]).then_inc(out_done, 16)
            sp.wait_ge(out_done, 16 * (NT // 2))

        @block.tensor
        def _(pe):
            pe.wait_ge(silu_c, 1)
            pe.wait_ge(c_wide, KD * NB)
            for j in range(6 * KD):
                for k in range(KD):
                    m = pe.matmul(PS[:, 0, NB * j:NB * j + NB], wmod_sb[:, k, P * j:P * j + P], sc[:, k, :],
                                  start=k == 0, stop=k == KD - 1)
            for b in range(NB):
                for i, which in enumerate((2, 5, 4, 3)):
                    for k in range(KD):
                        m = pe.matmul(PS[:, 1 + 2 * b + i // 2, DM * (i % 2):DM * (i % 2) + DM], sc_wide[:, k, b, :],
                                      wmod_sb[:, k, DM * which:DM * which + DM], start=k == 0, stop=k == KD - 1)
            m.then_inc(mod_mm, 1)

            pe.wait_ge(mod_step, 4)
            pe.sem_inc(h_done, 4)
            with pe.Fori(0, NB) as b:
                for j in range(2):
                    pe.wait_ge(xn_done, b * 8 + (4 * j + 4))
                    pe.wait_ge(h_done, b * 4 + (2 * j + 2))
                    for k in range(KD):
                        for t in range(4):
                            m = pe.transpose(PS[:, 4 + 2 * j + k, P * t:P * t + P], xn[:, j, t, P * k:P * k + P], ident[:, :])
                    m.then_inc(turned, 1)

            pe.wait_ge(w_in, 16 * 9)
            pe.wait_ge(h_done, 4 + 2 * 4)
            pe.sem_inc(six_copied, 1)
            pe.sem_inc(dt_free, 1)
            pe.sem_inc(xpad_done, 2)
            with pe.Fori(0, NB) as b:
                def project(bank, k_chunks, w, rhs, done):
                    for half in range(2):
                        for k in range(k_chunks):
                            m = pe.matmul(PS[:, bank + half, :], w(k), rhs(k, half), start=k == 0, stop=k == k_chunks - 1)
                    m.then_inc(done, 1)

                def h_cols(k, half):
                    return hT[:, k, bass.ds(b * L + half * HF, HF)]

                def six(use, w):
                    pe.wait_ge(six_copied, b * SIX + (use + 1))
                    project(6, KD, w, h_cols, six_mm)

                def x_of(c):
                    pe.wait_ge(xpad_done, b * CH + (c + 1))
                    project(2 * (c % 2), KD, lambda k: wx_sb[:, k, P * c:P * c + P], h_cols, x_mm)

                def dt_of(c):
                    if c == 0:
                        pe.wait_ge(six_copied, b * SIX + 2)
                    pe.wait_ge(dt_free, b * CH + (c + 1))
                    project(4, 1, lambda k: wdt_sb[:, P * c:P * c + P],
                            lambda k, half: dtd[:, HF * half:HF * half + HF], dt_mm)

                def C_of(c):
                    six(2 + c, lambda k: wC_sb[:, k, P * c:P * c + P])

                six(0, lambda k: wdd_sb[:, k, :])
                x_of(0)
                dt_of(0)
                x_of(1)
                six(1, lambda k: wB_sb[:, k, :])
                dt_of(1)
                C_of(0)
                x_of(2)
                x_of(3)
                dt_of(2)
                C_of(1)
                dt_of(3)
                C_of(2)
                C_of(3)
            pe.wait_ge(xpad_done, 2 + NB * CH)
            pe.sem_inc(sz_done, 2)
            with pe.Fori(0, NB) as b:
                for c in range(CH):
                    pe.wait_ge(sz_done, b * CH + (c + 1))
                    project(2 * (c % 2), KD, lambda k: wz_sb[:, k, P * c:P * c + P],
                            lambda k, half: hT[:, k, bass.ds(b * L + half * HF, HF)], z_mm)
            pe.drain().then_inc(a_over, 1)

            pe.wait_ge(sel_done, 1)
            pe.wait_ge(a_over, 4)
            pe.sem_inc(scan_done, 2)
            pe.sem_inc(dbu_done, 2)
            pe.sem_inc(exp_done, 1)
            pe.sem_inc(yev_done, 1)

            def front(g2, r, k):
                q, j = k // 4, k % 4
                n = g2 * (2 * NBK) + (r * NBK + k + 1)
                if k == 0:
                    pe.wait_ge(stk_in[r], g2 * 64 + 64)
                pe.wait_ge(dbu_done, n)
                for half in range(2):
                    m = pe.matmul(PS[:, 2 + 2 * (k % 2) + half, :], sel[0:96, j, :],
                                  stk[0:96, r, 1, q, HF * half:HF * half + HF], start=True, stop=True)
                m.then_inc(du_mm, 1)
                pe.wait_ge(exp_done, n)
                for half in range(2):
                    m = pe.matmul(PS[:, half, :], sel[0:96, j, :],
                                  stk[0:96, r, 0, q, HF * half:HF * half + HF], start=True, stop=True)
                m.then_inc(dl_mm, 1)
                if k == NBK - 1:
                    pe.wait_ge(dl_mm, n)
                    pe.sem_inc(stk_free, 1)

            def back(g2, r, k):
                j = r * NBK + k
                if j == 0:
                    pe.wait_ge(yev_done, g2 + 1)
                pe.wait_ge(prod_done, g2 * (2 * NBK) + (j + 1 + 2))
                for half in range(2):
                    m = pe.matmul(PS[:, 6 + half, :], ywide[:, P - BLK - BLK * j:2 * P - BLK - BLK * j],
                                  prod[:, k % 4, HF * half:HF * half + HF], start=j == 0, stop=j == 2 * NBK - 1)
                m.then_inc(ysum_done, 1)

            for k in range(LAG):
                front(0, 0, k)
            with pe.Fori(0, NG // 2 - 1) as g2:
                for r in range(2):
                    for k in range(NBK):
                        if k + LAG < NBK:
                            front(g2, r, k + LAG)
                        else:
                            front(g2 + r, 1 - r, k + LAG - NBK)
                        back(g2, r, k)
            for r in range(2):
                for k in range(NBK):
                    if k + LAG < NBK:
                        front(NG // 2 - 1, r, k + LAG)
                    elif r == 0:
                        front(NG // 2 - 1, 1, k + LAG - NBK)
                    back(NG // 2 - 1, r, k)
            pe.drain().then_inc(b_over, 1)

            pe.wait_ge(b_over, 4)
            with pe.Fori(0, NT // 2) as t:
                for j in range(2):
                    pe.wait_ge(v_done, t * 2 + (j + 1))
                    for k in range(CH):
                        m = pe.matmul(PS[:, j, 0:DM], v_st[:, j, k, :], wout_sb[:, k, :], start=k == 0, stop=k == CH - 1)
                    m.then_inc(o_mm, 1)
            pe.sem_inc(h2_done, 2)
            with pe.Fori(0, NT // 2) as t:
                for j in range(2):
                    pe.wait_ge(m_step, t * 4 + (2 * j + 2))
                    pe.wait_ge(h2_done, t * 2 + (j + 1))
                    for k in range(KD):
                        m = pe.transpose(PS[:, 2 + j, P * k:P * k + P], x2m[:, j, P * k:P * k + P], ident[:, :])
                    m.then_inc(h2_mm, 1)
                for j in range(2):
                    pe.wait_ge(h2_done, t * 2 + (j + 3))
                    for k in range(KD):
                        m = pe.matmul(PS[:, 4, bass.ds(t * (2 * NE) + j * NE, NE)], h2s[:, j, k, :], gate_sb[:, k, :],
                                      start=k == 0, stop=k == KD - 1)
                    m.then_inc(g_mm, 1)
            pe.wait_ge(route_step, ROUTE["picked"])
            pe.matmul(PS[:, 6, 0:NT * NE], tri, ohs, start=True, stop=True)
            pe.matmul(PS[:, 7, 0:NT * NE], ones, ohs, start=True, stop=True).then_inc(count_mm, 1)
            pe.drain().then_inc(c_over, 1)

            def turn(s2, r):
                pe.wait_ge(xg_in[r], s2 * 16 + 16)
                pe.wait_ge(xT_done, s2 * 2 + (r + 1))
                for k in range(KD):
                    m = pe.transpose(PS[:, 0, P * k:P * k + P], xg[:, r, P * k:P * k + P], ident[:, :])
                m.then_inc(xT_mm, 1)

            def expert_of(s2, r):
                return pe.value_load(etab[0:1, bass.ds(s2 * 2 + r, 1)], min_val=0, max_val=NE - 1)

            def hidden(s2, r):
                e = expert_of(s2, r)
                pe.wait_ge(xT_done, s2 * 2 + (r + 2))
                pe.wait_ge(inter_done, s2 * 2 + (r + 1))
                for bank, w, ready in ((2 + 2 * r, w0_sb, h0_mm), (3 + 2 * r, w1_sb, h01_mm)):
                    for k in range(KD):
                        m = pe.matmul(PS[:, bank, :], xgT[:, r, k, :],
                                      w[:, bass.ds(e, 1), k, :].rearrange("p e n -> p (e n)"), start=k == 0, stop=k == KD - 1)
                    m.then_inc(ready, 1)

            def turn_inter(s2, r):
                pe.wait_ge(inter_done, s2 * 2 + (r + 3))
                pe.wait_ge(iT_done, s2 * 2 + (r + 1))
                for k in range(KM):
                    m = pe.transpose(PS[:, 1, P * k:P * k + P], inter[:, r, P * k:P * k + P], ident[:, :])
                m.then_inc(iT_mm, 1)

            def outward(s2, r):
                e = expert_of(s2, r)
                pe.wait_ge(iT_done, s2 * 2 + (r + 2))
                pe.wait_ge(yo_done, s2 * 2 + (r + 1))
                for k in range(KM):
                    m = pe.matmul(PS[:, 6 + r, 0:DM], intT[:, r, k, :],
                                  wo_sb[:, bass.ds(e, 1), k, :].rearrange("p e n -> p (e n)"), start=k == 0, stop=k == KM - 1)
                m.then_inc(oe_mm, 1)

            pe.wait_ge(c_over, 4)
            pe.wait_ge(w01_in, 16 * 2 * NE)
            pe.wait_ge(wo_in, 16 * NE)
            pe.sem_inc(xT_done, 1)
            pe.sem_inc(inter_done, 2)
            pe.sem_inc(iT_done, 1)
            pe.sem_inc(yo_done, 2)
            turn(0, 0)
            turn(0, 1)
            hidden(0, 0)
            with pe.Fori(0, SPAIRS) as s2:
                for r in range(2):
                    turn(s2 + 1, r)
                    turn_inter(s2, r)
                    hidden(s2 + r, 1 - r)
                    outward(s2, r)
            turn(SPAIRS + 1, 0)
            turn_inter(SPAIRS, 0)
            hidden(SPAIRS, 1)
            outward(SPAIRS, 0)
            turn_inter(SPAIRS, 1)
            hidden(SPAIRS + 1, 0)
            outward(SPAIRS, 1)
            turn_inter(SPAIRS + 1, 0)
            outward(SPAIRS + 1, 0)

        @block.scalar
        def _(act):
            act.wait_ge(small_in, 16 * 8)
            act.activation(sc, cT_sb, ACT.Silu).then_inc(silu_c, 1)
            for b in range(NB):
                act.activation(negA[:, b, :], col[:, AL:NCOL], ACT.Exp).then_inc(col_done, 1)

            act.wait_ge(mod_step, 3)
            with act.Fori(0, NB) as b:
                for j in range(2):
                    act.wait_ge(turned, b * 2 + (j + 1 + 2))
                    for k in range(KD):
                        act.activation(hT[:, k, bass.ds(b * L + j * HF, HF)], PS[:, 4 + 2 * j + k, :], ACT.Identity,
                                       bias=modc[:, k, bass.ds(b, 1)], scale=modc[:, KD + k, bass.ds(b, 1)]).then_inc(h_done, 1)

            act.wait_ge(zero_done, 2)
            with act.Fori(0, NB) as b:
                def copy_six(use, dst):
                    act.wait_ge(six_mm, b * SIX + (use + 1))
                    act.activation(dst, pair(6), ACT.Copy).then_inc(six_copied, 1)

                def padded(c):
                    act.wait_ge(x_mm, b * CH + (c + 1))
                    if c >= 2:
                        act.wait_ge(conv_step, b * (CH * DC) + (c - 1) * DC)
                    act.activation(xpad[:, c % 2, DC - 1:DC - 1 + L], pair(2 * (c % 2)), ACT.Identity,
                                   bias=col[:, BX + c:BX + c + 1]).then_inc(xpad_done, 1)

                def silu_u(c):
                    act.wait_ge(conv_step, b * (CH * DC) + (c + 1) * DC)
                    act.activation(uT[:, bass.ds(b * CH + c, 1), :], acc[:, c % 2:c % 2 + 1, :], ACT.Silu,
                                   bias=col[:, CB + c:CB + c + 1]).then_inc(u_done, 1)

                def exp_abs(c):
                    act.wait_ge(dt_mm, b * CH + (c + 1))
                    act.wait_ge(r1_done, b * ITEMS + (2 * c + 1))
                    act.activation(spa[:, c % 2, :], pair(4), ACT.Abs, bias=bdt2[:, c:c + 1]).then_inc(sp_abs, 1)
                    act.wait_ge(sp_abs, b * CH + (c + 1))
                    act.activation(spa[:, c % 2, :], spa[:, c % 2, :], ACT.Exp, scale=-1.0).then_inc(sp_exp, 1)

                def ln_w(c):
                    act.wait_ge(sp_w, b * CH + (c + 1))
                    act.activation(spl[:, c % 2, :], spw[:, c % 2, :], ACT.Ln).then_inc(sp_ln, 1)

                def copy_C(c):
                    act.wait_ge(C_out[c % 2], b * 32 + 16 * (c // 2 + 1))
                    copy_six(2 + c, C_st[:, c % 2, :])

                def hi(i):
                    c = i // 2
                    act.wait_ge(parts_out[i % 4], b * 128 + 64 * (i // 4 + 1))
                    if i % 2 == 0:
                        act.wait_ge(delta_done, b * CH + (c + 1))
                        src = delta[:, c % 2, :]
                    else:
                        act.wait_ge(du_done, b * CH + (c + 1))
                        src = spa[:, c % 2, :]
                    act.activation(parts[:, i % 4, 0, :], src, ACT.Copy).then_inc(hi_done, 1)

                def mid(i):
                    act.wait_ge(r1_done, b * ITEMS + (i + 1 + 3))
                    act.activation(parts[:, i % 4, 1, :], r1[:, i % 2, :], ACT.Copy).then_inc(mid_done, 1)

                copy_six(0, dtd)
                padded(0)
                padded(1)
                exp_abs(0)
                act.wait_ge(B_out, b * 16 + 16)
                copy_six(1, B_st)
                exp_abs(1)
                padded(2)
                copy_C(0)
                ln_w(0)
                ln_w(1)
                padded(3)
                silu_u(0)
                silu_u(1)
                hi(0)
                hi(1)
                mid(0)
                exp_abs(2)
                hi(2)
                mid(1)
                hi(3)
                mid(2)
                exp_abs(3)
                mid(3)
                copy_C(1)
                ln_w(2)
                copy_C(2)
                ln_w(3)
                copy_C(3)
                silu_u(2)
                silu_u(3)
                hi(4)
                hi(5)
                mid(4)
                hi(6)
                mid(5)
                hi(7)
                mid(6)
                mid(7)
            act.wait_ge(B_out, 16 + 16 * NB)
            for r in range(2):
                act.wait_ge(C_out[r], 16 + 16 * NB * CH // 2)
            with act.Fori(0, NB) as b:
                for c in range(CH):
                    act.wait_ge(z_mm, b * CH + (c + 1))
                    act.activation(szT[:, bass.ds(b * CH + c, 1), :], pair(2 * (c % 2)), ACT.Silu,
                                   bias=col[:, BZ + c:BZ + c + 1]).then_inc(sz_done, 1)
            act.drain().then_inc(a_over, 1)

            act.wait_ge(a_over, 4)
            act.wait_ge(sels_in, 16)
            act.activation(sel[0:96], sels_f[0:96], ACT.Copy).then_inc(sel_done, 1)
            act.sem_inc(prod_done, 2)
            decay = negA[:, :, :].rearrange("p b n -> p (b n)")
            with act.Fori(0, NG // 2) as g2:
                for n in range(2 * NBK):
                    act.wait_ge(dl_mm, g2 * (2 * NBK) + (n + 1))
                    act.wait_ge(scan_done, g2 * (2 * NBK) + (n + 1))
                    act.activation(da[:, n % 2, :], pair(0), ACT.Exp,
                                   scale=decay[:, bass.ds(g2 * (2 * NBK) + n, 1)]).then_inc(exp_done, 1)
            act.drain().then_inc(b_over, 1)

            act.wait_ge(b_over, 4)
            act.sem_inc(g_mm, 2)
            with act.Fori(0, NT // 2) as t:
                for j in range(2):
                    act.wait_ge(h2_mm, t * 2 + (j + 3))
                    act.wait_ge(g_mm, t * 2 + (j + 1))
                    act.activation(h2s[:, j], PS[:, 2 + j, 0:DM].rearrange("p (k n) -> p k n", k=KD), ACT.Copy).then_inc(h2_done, 1)
            act.wait_ge(route_step, ROUTE["gap"])
            act.activation(w12[:, 1, :], w12[:, 0, :], ACT.Exp).then_inc(ex_done, 1)
            act.drain().then_inc(c_over, 1)

            def take_rows(s2, r):
                act.wait_ge(xT_mm, s2 * 2 + (r + 1))
                act.wait_ge(h01_mm, s2 * 2 + (r + 1))
                act.activation(xgT[:, r], PS[:, 0, 0:DM].rearrange("p (k n) -> p k n", k=KD),
                               ACT.Copy).then_inc(xT_done, 1)

            def silu_h(s2, r):
                act.wait_ge(h0_mm, s2 * 2 + (r + 1))
                act.wait_ge(inter_done, s2 * 2 + (r + 1))
                act.activation(sil[:, r, :], PS[:, 2 + 2 * r, :], ACT.Silu).then_inc(sil_done, 1)

            def leave(s2, r):
                act.wait_ge(oe_mm, s2 * 2 + (r + 3))
                act.wait_ge(yo_out[r], s2 * 16 + 16)
                act.activation(yo[:, r, :], PS[:, 6 + r, 0:DM], ACT.Copy).then_inc(yo_done, 1)
                act.wait_ge(yo_done, s2 * 2 + (r + 3))
                act.dma_start(ys_dram[bass.ds(s2 * (2 * P) + r * P, P), :], yo[:, r, :]).then_inc(yo_out[r], 16)

            act.wait_ge(c_over, 4)
            act.sem_inc(h01_mm, 2)
            for r in range(2):
                act.sem_inc(yo_out[r], 16)
            take_rows(0, 0)
            take_rows(0, 1)
            silu_h(0, 0)
            with act.Fori(0, SPAIRS) as s2:
                for r in range(2):
                    take_rows(s2 + 1, r)
                    silu_h(s2 + r, 1 - r)
                    leave(s2, r)
            take_rows(SPAIRS + 1, 0)
            silu_h(SPAIRS, 1)
            leave(SPAIRS, 0)
            silu_h(SPAIRS + 1, 0)
            leave(SPAIRS, 1)
            leave(SPAIRS + 1, 0)

            for t in range(NT):
                act.wait_ge(got[t // 2], 16 * 4)
                act.activation(back_rows[:, 1, t, :], back_rows[:, 1, t, :], ACT.Copy, scale=w12[:, 3, t:t + 1]).then_inc(weighed, 1)

        @block.vector
        def _(dve):
            dve.wait_ge(small_in, 16 * 8)
            dve.wait_ge(silu_c, 1)
            for k in range(KD):
                for b in range(NB):
                    dve.tensor_scalar(sc_wide[:, k, b, :], ident[:, :], 0.0, sc[:, k, b:b + 1], ALU.mult, ALU.add).then_inc(c_wide, 1)
            dve.memset(zrow[:, :], 0.0).then_inc(zero_rows, 1)
            for b in range(NB):
                dve.tensor_copy(Dcol[:, CH * b:CH * b + CH], col[:, DD:DD + CH]).then_inc(d_done, 1)
            dve.memset(xpad[:, :, 0:DC - 1], 0.0).then_inc(zero_done, 1)
            dve.tensor_scalar(bdt2[:, :], col[:, BDT:BDT + CH], 2.0, None, ALU.mult).then_inc(zero_done, 1)

            dve.wait_ge(col_done, NB)
            dve.tensor_scalar(negA[:, :, :], negA[:, :, :], -1.0, None, ALU.mult).then_inc(col_done, 1)

            dve.wait_ge(x_in, 16)
            with dve.Fori(0, NT) as t:
                dve.bn_stats(stat[:, bass.ds(t, 1), :], x_tok[:, bass.ds(t, 1), :]).then_inc(stat_done, 1)
            dve.wait_ge(stat_done, NT)
            for t in range(NT):
                dve.bn_aggr(mv[:, t, :], stat[:, t, :]).then_inc(aggr_done, 1)

            dve.wait_ge(mod_mm, 1)
            dve.tensor_copy(modc[:, :, :], PS[:, 0, 0:6 * KD * NB].rearrange("p (j b) -> p j b", b=NB)).then_inc(mod_step, 1)
            dve.wait_ge(mod_step, 1)
            for n, j in ((1, KD), (2, 4 * KD)):
                dve.tensor_scalar(modc[:, j:j + KD, :], modc[:, j:j + KD, :], 1.0, None, ALU.add).then_inc(mod_step, 1)
            dve.tensor_copy(grow[:, :, :, :].rearrange("p b i n -> p (b i n)"),
                            PS[:, 1:5, :].rearrange("p a n -> p (a n)")).then_inc(mod_step, 1)
            dve.wait_ge(mod_step, 4)
            gates = grow[:, :, 0:2, :].rearrange("p b i n -> p b (i n)")
            dve.tensor_scalar(grow[:, :, 2, :], grow[:, :, 2, :], 1.0, None, ALU.add).then_inc(mod_step, 1)
            dve.tensor_scalar(gate_tmp[:, 0], gates, 0.0, 2.0, ALU.is_ge, ALU.mult).then_inc(mod_step, 1)
            dve.scalar_tensor_tensor(gate_tmp[:, 1], gates, -1.0, gates, ALU.mult, ALU.max).then_inc(mod_step, 1)
            dve.wait_ge(mod_step, 7)
            dve.tensor_scalar(gate_tmp[:, 1], gate_tmp[:, 1], 0.25, None, ALU.max).then_inc(mod_step, 1)
            dve.wait_ge(mod_step, 8)
            dve.scalar_tensor_tensor(gates, gate_tmp[:, 0], -1.0, gate_tmp[:, 1], ALU.add, ALU.mult).then_inc(mod_step, 1)

            dve.wait_ge(rstd_done, 2)
            dve.sem_inc(turned, 2)
            with dve.Fori(0, NB) as b:
                for j in range(2):
                    dve.wait_ge(turned, b * 2 + (j + 1))
                    for t in range(4):
                        at = b * NTB + (4 * j + t)
                        dve.tensor_scalar(xn[:, j, t:t + 1, :], x_tok[:, bass.ds(at, 1), :], mv[:, bass.ds(at, 1), 0],
                                          rstd[:, bass.ds(at, 1)], ALU.subtract, ALU.mult).then_inc(xn_done, 1)

            dve.sem_inc(u_done, 2)
            dve.sem_inc(r1_done, 3)
            dve.sem_inc(lo_done, 2)
            with dve.Fori(0, NB) as b:
                def conv(c):
                    dve.wait_ge(xpad_done, b * CH + (c + 3))
                    dve.wait_ge(u_done, b * CH + (c + 1))
                    for k in range(DC):
                        tap = col[:, CW + DC * c + k:CW + DC * c + k + 1]
                        if k == 0:
                            dve.tensor_scalar(acc[:, c % 2, :], xpad[:, c % 2, k:k + L], tap, None, ALU.mult).then_inc(conv_step, 1)
                        else:
                            dve.wait_ge(conv_step, b * (CH * DC) + (c * DC + k))
                            dve.scalar_tensor_tensor(acc[:, c % 2, :], xpad[:, c % 2, k:k + L], tap, acc[:, c % 2, :],
                                                     ALU.mult, ALU.add).then_inc(conv_step, 1)

                def one_plus(c):
                    dve.wait_ge(sp_exp, b * CH + (c + 1))
                    dve.tensor_scalar(spw[:, c % 2, :], spa[:, c % 2, :], 1.0, None, ALU.add).then_inc(sp_w, 1)
                    dve.tensor_scalar(delta[:, c % 2, :], pair(4), bdt2[:, c:c + 1], 0.0, ALU.add, ALU.max).then_inc(dt_free, 1)

                def rounding(c):
                    dve.wait_ge(sp_ln, b * CH + (c + 1))
                    dve.scalar_tensor_tensor(spw[:, c % 2, :], spw[:, c % 2, :], -1.0, spa[:, c % 2, :],
                                             ALU.add, ALU.subtract).then_inc(sp_k, 1)

                def delta_of(c):
                    dve.wait_ge(sp_sub, b * CH + (c + 1))
                    dve.tensor_tensor(spl[:, c % 2, :], spl[:, c % 2, :], spa[:, c % 2, :], ALU.min).then_inc(sp_min, 1)
                    dve.wait_ge(sp_min, b * CH + (c + 1))
                    dve.wait_ge(dt_free, b * CH + (c + 2))
                    dve.tensor_tensor(delta[:, c % 2, :], spl[:, c % 2, :], delta[:, c % 2, :], ALU.add).then_inc(delta_done, 1)

                def rest(i):
                    src = delta if i % 2 == 0 else spa
                    dve.wait_ge(hi_done, b * ITEMS + (i + 1))
                    dve.wait_ge(lo_done, b * ITEMS + (i + 1))
                    dve.tensor_tensor(r1[:, i % 2, :], src[:, i // 2 % 2, :], parts[:, i % 4, 0, :],
                                      ALU.subtract).then_inc(r1_done, 1)

                conv(0)
                one_plus(0)
                conv(1)
                one_plus(1)
                rounding(0)
                conv(2)
                rounding(1)
                delta_of(0)
                delta_of(1)
                conv(3)
                rest(0)
                rest(1)
                rest(2)
                one_plus(2)
                rest(3)
                one_plus(3)
                rounding(2)
                rounding(3)
                delta_of(2)
                delta_of(3)
                for i in range(4, 8):
                    rest(i)
            dve.drain().then_inc(a_over, 1)

            dve.wait_ge(a_over, 4)

            def drive(g2, r, k):
                n = r * NBK + k
                if k == 0:
                    dve.wait_ge(brep_in[r], g2 * 16 + 16)
                dve.wait_ge(du_mm, g2 * (2 * NBK) + (n + 1))
                dve.wait_ge(scan_done, g2 * (2 * NBK) + (n + 1))
                dve.tensor_tensor(dbu[:, k % 2, :], pair(2 + 2 * (k % 2)), brep[:, r, :], ALU.mult).then_inc(dbu_done, 1)

            def scan(g2, r, k):
                n = r * NBK + k
                dve.wait_ge(exp_done, g2 * (2 * NBK) + (n + 2))
                dve.wait_ge(dbu_done, g2 * (2 * NBK) + (n + 3))
                dve.wait_ge(prod_done, g2 * (2 * NBK) + (n + 1))
                dve.tensor_tensor_scan(hst[:, k % 2, :], da[:, k % 2, :], dbu[:, k % 2, :], 0.0,
                                       ALU.mult, ALU.add).then_inc(scan_done, 1)

            def leave(g2):
                dve.wait_ge(ysum_done, g2 * (2 * NBK) + 4 * NBK)
                chunk = uT[:, bass.ds(g2, 1), :].rearrange("p c n -> p (c n)")
                dve.scalar_tensor_tensor(chunk, chunk, Dcol[:, bass.ds(g2, 1)], pair(6), ALU.mult, ALU.add).then_inc(yev_done, 1)

            def chunk_of_blocks(g2, first):
                for r in range(2):
                    drive(g2, r, 0)
                    for k in range(1, NBK):
                        drive(g2, r, k)
                        scan(g2, r, k - 1)
                        if r == 0 and k == LAG and not first:
                            leave(g2 - 1)
                    scan(g2, r, NBK - 1)

            chunk_of_blocks(0, True)
            with dve.Fori(1, NG // 2) as g2:
                chunk_of_blocks(g2, False)
            leave(NG // 2 - 1)
            dve.drain().then_inc(b_over, 1)

            dve.wait_ge(b_over, 4)
            y4 = uT[:, :, :].rearrange("p (b c) n -> p b c n", b=NB)
            sz4 = szT.rearrange("p (b c) n -> p b c n", b=NB)
            dve.sem_inc(o_mm, 2)
            with dve.Fori(0, NB) as b:
                def gated(t, j):
                    def tokens(a):
                        return a[:, bass.ds(b, 1), :, bass.ds(t * (2 * P) + j * P, P)].rearrange("p b c n -> p (b c) n")

                    dve.wait_ge(o_mm, b * NTB + t * 2 + (j + 1))
                    dve.tensor_tensor(v_st[:, j], tokens(y4), tokens(sz4), ALU.mult).then_inc(v_done, 1)

                def attended(t, j, following):
                    rows_j = x_tok[:, bass.ds(b * NTB + t * 2 + j, 1), :]
                    at = b * (4 * NTB) + t * 8 + 4 * j
                    dve.wait_ge(o_mm, b * NTB + t * 2 + (j + 3))
                    dve.tensor_tensor(x2n[:, j, :], PS[:, j, 0:DM], row[:, :], ALU.add).then_inc(x2_step, 1)
                    if following:
                        gated(t + 1, j)
                    dve.wait_ge(x2_step, at + 1)
                    dve.tensor_tensor(x2n[:, j:j + 1, :], x2n[:, j:j + 1, :], grow[:, bass.ds(b, 1), 0, :], ALU.mult).then_inc(x2_step, 1)
                    dve.wait_ge(x2_step, at + 2)
                    dve.tensor_tensor(rows_j, rows_j, x2n[:, j:j + 1, :], ALU.add).then_inc(x2_step, 1)
                    dve.wait_ge(x2_step, at + 3)
                    dve.sem_inc(passed, 1)
                    dve.bn_stats(stat[:, bass.ds(b * NTB + t * 2 + j, 1), :], rows_j).then_inc(x2_step, 1)

                gated(0, 0)
                gated(0, 1)
                with dve.Fori(0, NTB // 2 - 1) as t:
                    attended(t, 0, True)
                    attended(t, 1, True)
                attended(NTB // 2 - 1, 0, False)
                attended(NTB // 2 - 1, 1, False)
            dve.wait_ge(x2_step, 4 * NT)
            for t in range(NT):
                dve.bn_aggr(mv[:, t, :], stat[:, t, :]).then_inc(aggr2_done, 1)

            dve.wait_ge(rstd2_done, 2)
            dve.sem_inc(h2_mm, 2)
            dve.sem_inc(kept, 2)
            with dve.Fori(0, NB) as b:
                with dve.Fori(0, NTB // 2) as t:
                    for j in range(2):
                        tile = b * NTB + t * 2 + j
                        row_j = slice(j, j + 1)
                        dve.scalar_tensor_tensor(x2n[:, row_j, :], x_tok[:, bass.ds(tile, 1), :], mv[:, bass.ds(tile, 1), 0],
                                                 grow[:, bass.ds(b, 1), 2, :], ALU.subtract, ALU.mult).then_inc(m_step, 1)
                        dve.wait_ge(m_step, b * (2 * NTB) + t * 4 + (2 * j + 1))
                        dve.wait_ge(h2_mm, b * NTB + t * 2 + (j + 1))
                        dve.wait_ge(kept, b * NTB + t * 2 + (j + 1))
                        dve.scalar_tensor_tensor(x2m[:, row_j, :], x2n[:, row_j, :], rstd[:, bass.ds(tile, 1)],
                                                 grow[:, bass.ds(b, 1), 3, :], ALU.mult, ALU.add).then_inc(m_step, 1)

            route = [0]

            def step(ins):
                ins.then_inc(route_step, 1)
                route[0] += 1

            def settled():
                dve.wait_ge(route_step, route[0])

            dve.wait_ge(g_mm, 2 + NT)
            step(dve.tensor_copy(lgt.rearrange("p t n -> p (t n)"), PS[:, 4, 0:NT * NE]))
            step(dve.tensor_copy(tri, tri_f[:, :]))
            step(dve.memset(ones, 1.0))
            settled()
            for t in range(NT):
                dve.max(top8[:, t, :], lgt[:, t, :]).then_inc(max_done, 1)
            for t in range(NT):
                dve.wait_ge(max_done, t + 1)
                dve.max_index(i8[:, t, :], top8[:, t, :], lgt[:, t, :]).then_inc(index_done, 1)
            dve.wait_ge(index_done, NT)
            step(dve.tensor_copy(idxf, i8))
            step(dve.tensor_tensor(w12[:, 0, :], top8[:, :, 1], top8[:, :, 0], ALU.subtract))
            assert route[0] == ROUTE["gap"]
            settled()
            for i in range(2):
                step(dve.tensor_tensor(oh[:, i], iota8[:, :].unsqueeze(1).broadcast_to([P, NT, NE]),
                                       idxf[:, :, i:i + 1].broadcast_to([P, NT, NE]), ALU.is_equal))
            settled()
            step(dve.tensor_tensor(ohs, oh[:, 0].rearrange("p t n -> p (t n)"), oh[:, 1].rearrange("p t n -> p (t n)"), ALU.add))
            assert route[0] == ROUTE["picked"]
            dve.wait_ge(count_mm, 1)
            step(dve.tensor_copy(tots.rearrange("p t n -> p (t n)"), PS[:, 7, 0:NT * NE]))
            step(dve.memset(pre[:, 0, :], 0.0))
            for t in range(NT):
                settled()
                step(dve.tensor_tensor(pre[:, t + 1, :], pre[:, t, :], tots[:, t, :], ALU.add))
            settled()
            step(dve.tensor_scalar(cnti, pre[:, NT, :], float(P - 1), None, ALU.add))
            settled()
            step(dve.tensor_scalar(cnti, cnti, 7, None, ALU.arith_shift_right))
            settled()
            step(dve.tensor_copy(cnt, cnti))
            step(dve.memset(off[:, 0:1], 0.0))
            for e in range(NE - 1):
                settled()
                step(dve.tensor_tensor(off[:, e + 1:e + 2], off[:, e:e + 1], cnt[:, e:e + 1], ALU.add))
            settled()
            step(dve.tensor_scalar(offr, off[:, 0:NE], float(P), None, ALU.mult))
            step(dve.tensor_scalar(ef, iota_s[:, :], off[:, 1:2], None, ALU.is_ge))
            step(dve.tensor_tensor(place, PS[:, 6, 0:NT * NE].rearrange("p (t n) -> p t n", n=NE), pre[:, 0:NT, :], ALU.add))
            for e in range(2, NE):
                settled()
                step(dve.scalar_tensor_tensor(ef, iota_s[:, :], off[:, e:e + 1], ef, ALU.is_ge, ALU.add))
            settled()
            step(dve.tensor_copy(etab[:, :], ef))
            step(dve.tensor_tensor(place, place, offr.unsqueeze(1).broadcast_to([P, NT, NE]), ALU.add))
            settled()
            for i in range(2):
                step(dve.tensor_tensor(ohp[:, i], oh[:, i], place, ALU.mult))
            settled()
            for i in range(2):
                step(dve.tensor_reduce(posf[:, i, :], ohp[:, i], AX.X, ALU.add))
            settled()
            step(dve.tensor_copy(posu[:, :, :], posf))
            settled()
            dve.sem_inc(placed, 1)
            dve.wait_ge(ex_done, 1)
            step(dve.tensor_scalar(w12[:, 2, :], w12[:, 1, :], 1.0, None, ALU.add))
            settled()
            step(dve.reciprocal(w12[:, 2, :], w12[:, 2, :]))
            settled()
            step(dve.tensor_tensor(w12[:, 3, :], w12[:, 1, :], w12[:, 2, :], ALU.mult))
            settled()
            dve.drain().then_inc(c_over, 1)

            def gate_h(s2, r):
                dve.wait_ge(sil_done, s2 * 2 + (r + 1))
                dve.wait_ge(h01_mm, s2 * 2 + (r + 3))
                dve.wait_ge(iT_mm, s2 * 2 + (r + 1))
                dve.tensor_tensor(inter[:, r, :], sil[:, r, :], PS[:, 3 + 2 * r, :], ALU.mult).then_inc(inter_done, 1)

            def take_inter(s2, r):
                dve.wait_ge(iT_mm, s2 * 2 + (r + 3))
                dve.wait_ge(oe_mm, s2 * 2 + (r + 1))
                dve.tensor_copy(intT[:, r].rearrange("p k n -> p (k n)"), PS[:, 1, :]).then_inc(iT_done, 1)

            dve.wait_ge(c_over, 4)
            dve.sem_inc(iT_mm, 2)
            dve.sem_inc(oe_mm, 2)
            gate_h(0, 0)
            with dve.Fori(0, SPAIRS) as s2:
                for r in range(2):
                    take_inter(s2, r)
                    gate_h(s2 + r, 1 - r)
            take_inter(SPAIRS, 0)
            gate_h(SPAIRS, 1)
            take_inter(SPAIRS, 1)
            gate_h(SPAIRS + 1, 0)
            take_inter(SPAIRS + 1, 0)

            for t in range(NT):
                mine = back_rows[:, 0, t, :]
                dve.wait_ge(weighed, t + 1)
                step(dve.scalar_tensor_tensor(mine, mine, w12[:, 2, t:t + 1], back_rows[:, 1, t, :], ALU.mult, ALU.add))
                settled()
                step(dve.tensor_tensor(mine, mine, grow[:, t // NTB, 1, :], ALU.mult))
                settled()
                dve.tensor_tensor(x_tok[:, t, :], x_tok[:, t, :], mine, ALU.add).then_inc(fin_done, 1)

        @block.gpsimd
        def _(gp):
            gp.memset(nhalf[:, :], -0.5).then_inc(nhalf_done, 1)
            gp.wait_ge(nhalf_done, 1)
            gp.wait_ge(aggr_done, NT)
            gp.tensor_scalar(rstd[:, :], mv[:, :, 1], EPS, None, ALU.add).then_inc(rstd_done, 1)
            gp.wait_ge(rstd_done, 1)
            gp.tensor_tensor(rstd[:, :], rstd[:, :], nhalf[:, :], ALU.pow).then_inc(rstd_done, 1)

            with gp.Fori(0, NB) as b:
                def corrected(c):
                    gp.wait_ge(sp_k, b * CH + (c + 1))
                    gp.tensor_tensor(spl[:, c % 2, :], spl[:, c % 2, :], spw[:, c % 2, :], ALU.subtract).then_inc(sp_sub, 1)

                def times_u(c):
                    gp.wait_ge(delta_done, b * CH + (c + 1))
                    gp.wait_ge(u_done, b * CH + (c + 3))
                    gp.tensor_tensor(spa[:, c % 2, :], delta[:, c % 2, :],
                                     uT[:, bass.ds(b * CH + c, 1), :].rearrange("p c n -> p (c n)"), ALU.mult).then_inc(du_done, 1)

                def low(i):
                    gp.wait_ge(mid_done, b * ITEMS + (i + 1))
                    gp.tensor_tensor(parts[:, i % 4, 2, :], r1[:, i % 2, :], parts[:, i % 4, 1, :], ALU.subtract).then_inc(lo_done, 1)

                for c in range(0, CH, 2):
                    corrected(c)
                    corrected(c + 1)
                    times_u(c)
                    times_u(c + 1)
                    for i in range(4):
                        low(2 * c + i)
            gp.drain().then_inc(a_over, 1)

            gp.wait_ge(a_over, 4)
            with gp.Fori(0, NG) as g:
                for k in range(NBK):
                    gp.wait_ge(scan_done, g * NBK + (k + 3))
                    if k % 2 == 0:
                        gp.wait_ge(crep_in[k // 2], g * 16 + 16)
                    gp.wait_ge(ysum_done, g * NBK + (k + 1 + 2 * NBK - 4))
                    gp.tensor_tensor(prod[:, k % 4, :], hst[:, k % 2, :], crep[:, k // 2, :], ALU.mult).then_inc(prod_done, 1)
            gp.drain().then_inc(b_over, 1)

            gp.wait_ge(b_over, 4)
            gp.wait_ge(aggr2_done, NT)
            gp.tensor_scalar(rstd[:, :], mv[:, :, 1], EPS, None, ALU.add).then_inc(rstd2_done, 1)
            gp.wait_ge(rstd2_done, 1)
            gp.tensor_tensor(rstd[:, :], rstd[:, :], nhalf[:, :], ALU.pow).then_inc(rstd2_done, 1)
            with gp.Fori(0, NT // 2) as t:
                for j in range(2):
                    gp.wait_ge(m_step, t * 4 + (2 * j + 2))
                    gp.sem_inc(passed, 1)
                    gp.tensor_copy(h2row[:, bass.ds(t * 2 + j, 1), :], x2m[:, j:j + 1, :]).then_inc(kept, 1)
            gp.wait_ge(kept, 2 + NT)
            gp.drain().then_inc(c_over, 1)

            gp.wait_ge(placed, 1)
            gp.wait_ge(xs_zeroed, 16 * NS // ZS)
            for t in range(NT):
                for i in range(2):
                    gp.indirect_dma_start(out=xs_dram, out_offset=bass.IndirectOffsetOnAxis(ap=posu[:, i, t:t + 1], axis=0),
                                          in_=h2row[:, t, :], in_offset=None).then_inc(sent, 16)
            gp.wait_ge(yo_out[0], 16 + 16 * (NS // 2 + 1))
            gp.wait_ge(yo_out[1], 16 + 16 * (NS // 2))
            for t in range(NT):
                for i in range(2):
                    gp.indirect_dma_start(out=back_rows[:, i, t, :], out_offset=None, in_=ys_dram,
                                          in_offset=bass.IndirectOffsetOnAxis(ap=posu[:, i, t:t + 1], axis=0)
                                          ).then_inc(got[t // 2], 16)


def kernel(**inputs):
    import numpy as _np
    import concourse.bacc as _bacc
    from concourse import mybir as _mybir
    from concourse.bass_utils import run_bass_kernel_spmd as _run

    a = {k[3:]: _np.asarray(v) for k, v in inputs.items()}
    at = {k.replace("attn_", ""): v for k, v in a.items()}

    def by_channel(v):
        v = v.reshape(CH, P, -1)
        return v.transpose(1, 0, 2).reshape(P, -1)

    def repeated(v):
        v = v.reshape(DXB // DS, 1, DS, -1)
        return _np.broadcast_to(v, (DXB // DS, DIN // DXB, DS, v.shape[-1])).reshape(DIN, -1)

    cols = _np.concatenate([by_channel(repeated(at["bx"])), by_channel(at["conv_b"]), by_channel(at["bdt"]),
                            by_channel(at["D"]), by_channel(at["bz"]), by_channel(at["conv_w"].reshape(DIN, DC)),
                            at["A_log"].reshape(DIN // BLK, BLK, DS).transpose(2, 1, 0).reshape(P, -1)], axis=1)
    rows = _np.broadcast_to(at["bout"][None], (P, DM))

    consts = _np.zeros((P, CTRI + P), _np.float32)
    consts[:, :P] = _np.eye(P)
    consts[:, CI8:CI8 + NE] = _np.arange(NE)
    consts[:, CIS:CIS + NS] = _np.arange(NS)
    consts[_np.arange(P), CYW + P - BLK + _np.arange(P) % BLK] = 1
    consts[:, CTRI:] = _np.triu(_np.ones((P, P)), 1)
    sels = _np.zeros((32 * PARTS, 4, P), _np.float32)
    m = _np.arange(P)
    for part in range(PARTS):
        for j in range(4):
            sels[32 * part + BLK * j + m % BLK, j, m] = 1

    arrays = {
        "x": at["hidden_states"].reshape(T, DM), "cols": cols, "rows": rows, "consts": consts, "sels": sels.reshape(96, -1),
        "cT": a["c"].T, "wmod": a["wmod"], "wx": repeated(at["Wx"]).T, "wz": at["Wz"].T, "wB": at["WB"].T, "wC": at["WC"].T,
        "wdd": at["Wdt_down"].T, "wdt": at["Wdt"].T, "wout": at["Wout"].T, "gate": a["ffn_gate_kernel"],
        "w0": a["ffn_w0_kernel"], "w1": a["ffn_w1_kernel"], "wo": a["ffn_wo_kernel"],
    }
    nc = _bacc.Bacc("TRN2", target_bir_lowering=False, num_devices=1)
    args, feeds = [], {}
    for name, v in arrays.items():
        v = _np.ascontiguousarray(v)
        feeds[f"in_{name}"] = v
        args.append(nc.dram_tensor(f"in_{name}", v.shape, _mybir.dt.from_np(v.dtype), kind="ExternalInput").ap())
    args.append(nc.dram_tensor("out", (T, DM), _mybir.dt.float32, kind="ExternalOutput").ap())
    adaln_mamba_moe(nc, *args)
    r = _run(nc, [feeds], core_ids=[0])
    return r.results[0]["out"].reshape(NB, L, DM)
```
